# Optimizing a Trainium2 kernel written in Bass

```python
import numpy as np
import jax
import jax.numpy as jnp

def _softmax(x, axis=-1):
    return jax.nn.softmax(x, axis=axis)

def _gelu(x):
    return jax.nn.gelu(x, approximate=True)

def _silu(x):
    return jax.nn.silu(x)

def _sigmoid(x):
    return jax.nn.sigmoid(x)

def _layernorm(x, axis=-1, eps=1e-05):
    m = jnp.mean(x, axis=axis, keepdims=True)
    v = jnp.var(x, axis=axis, keepdims=True)
    return (x - m) / jnp.sqrt(v + eps)

def _scatter_add(tgt, idx, src, axis=0):
    return tgt.at[idx].add(src)

def _segment_sum(src, seg, n):
    return jax.ops.segment_sum(src, seg, n)
kernel_name = 'mk_gnn_resnorm_d1_gnn_r8_422397'

def setup_inputs(seed: int=0):
    np.random.seed(seed)
    _w = jnp.asarray

    def _rec_inputs():
        import jax
        import jax.numpy as jnp
        _gk = jax.random.key(seed)
        x = -6.415e-05 + 1 * jax.random.normal(jax.random.fold_in(_gk, 1), (1250, 512), jnp.float32)
        src = jax.random.randint(jax.random.fold_in(_gk, 2), (40000,), 0, 1250, jnp.int32)
        dst = jax.random.randint(jax.random.fold_in(_gk, 3), (40000,), 0, 1250, jnp.int32)
        _o = jnp.argsort(dst, stable=True)
        src = src[_o]
        dst = dst[_o]
        edge_weight1 = -0.00598325 + 0.997157 * jax.random.normal(jax.random.fold_in(_gk, 12), (40000, 1), jnp.float32)
        return (x, src, dst, edge_weight1)
    x, src, dst, edge_weight1 = _rec_inputs()

    def _L0_gnn_setup():
        import jax, jax.numpy as jnp
        import numpy as np
        N, D, E, L = (2500, 512, 20000, 4)
        BN_EPS = 1e-05

        def _gine_layer(x, src, dst, edge_attr, eps, We, be, W1, b1, gamma, beta, W2, b2):
            e = edge_attr @ We + be
            m = jax.nn.relu(x[src] + e)
            agg = jax.ops.segment_sum(m, dst, num_segments=x.shape[0])
            h = ((1.0 + eps) * x + agg) @ W1 + b1
            mu = jnp.mean(h, axis=0)
            var = jnp.mean(jnp.square(h - mu), axis=0)
            h = (h - mu) * jax.lax.rsqrt(var + BN_EPS) * gamma + beta
            h = jax.nn.relu(h)
            return jax.nn.relu(h @ W2 + b2)
        key = jax.random.key(seed)
        ks = jax.random.split(key, 10)
        x = jax.random.normal(ks[0], (N, D), dtype=jnp.float32)
        edge_index = jax.random.randint(ks[1], (2, E), 0, N, dtype=jnp.int64)
        edge_attr = jax.random.normal(ks[2], (E, 1), dtype=jnp.float32)
        s1 = 1.0 / np.sqrt(D)
        params = {'eps': jnp.zeros((L,), jnp.float32), 'We': jax.random.normal(ks[3], (L, 1, D), jnp.float32) * 1.0, 'be': jnp.zeros((L, D), jnp.float32), 'W1': jax.random.normal(ks[4], (L, D, D), jnp.float32) * s1, 'b1': jnp.zeros((L, D), jnp.float32), 'gamma': jnp.ones((L, D), jnp.float32), 'beta': jnp.zeros((L, D), jnp.float32), 'W2': jax.random.normal(ks[5], (L, D, D), jnp.float32) * s1, 'b2': jnp.zeros((L, D), jnp.float32)}
        return {'x': x, 'edge_index': edge_index, 'edge_attr': edge_attr, **params}
    _L0_gnn_all = _L0_gnn_setup()
    _L0_gnn_in = {k: v for k, v in _L0_gnn_all.items() if k in ('eps', 'We', 'be', 'W1', 'b1', 'gamma', 'beta', 'W2', 'b2')}
    del _L0_gnn_all
    return {'x': x, 'src': src, 'dst': dst, 'edge_weight1': edge_weight1, 'L0_gnn_eps': _L0_gnn_in['eps'], 'L0_gnn_We': _L0_gnn_in['We'], 'L0_gnn_be': _L0_gnn_in['be'], 'L0_gnn_W1': _L0_gnn_in['W1'], 'L0_gnn_b1': _L0_gnn_in['b1'], 'L0_gnn_gamma': _L0_gnn_in['gamma'], 'L0_gnn_beta': _L0_gnn_in['beta'], 'L0_gnn_W2': _L0_gnn_in['W2'], 'L0_gnn_b2': _L0_gnn_in['b2']}

def reference(x, src, dst, edge_weight1, L0_gnn_eps, L0_gnn_We, L0_gnn_be, L0_gnn_W1, L0_gnn_b1, L0_gnn_gamma, L0_gnn_beta, L0_gnn_W2, L0_gnn_b2):
    import jax
    import jax.numpy as jnp

    def _L0_gnn_ref(x, edge_index, edge_attr, eps, We, be, W1, b1, gamma, beta, W2, b2):
        import jax, jax.numpy as jnp
        import numpy as np
        N, D, E, L = (2500, 512, 20000, 4)
        BN_EPS = 1e-05

        def _gine_layer(x, src, dst, edge_attr, eps, We, be, W1, b1, gamma, beta, W2, b2):
            e = edge_attr @ We + be
            m = jax.nn.relu(x[src] + e)
            agg = jax.ops.segment_sum(m, dst, num_segments=x.shape[0])
            h = ((1.0 + eps) * x + agg) @ W1 + b1
            mu = jnp.mean(h, axis=0)
            var = jnp.mean(jnp.square(h - mu), axis=0)
            h = (h - mu) * jax.lax.rsqrt(var + BN_EPS) * gamma + beta
            h = jax.nn.relu(h)
            return jax.nn.relu(h @ W2 + b2)
        src, dst = (edge_index[0], edge_index[1])
        for l in range(L):
            x = _gine_layer(x, src, dst, edge_attr, eps[l], We[l], be[l], W1[l], b1[l], gamma[l], beta[l], W2[l], b2[l])
        return x
    edge_index = jnp.stack([src, dst])
    x = _layernorm(x + _L0_gnn_ref(x, edge_index, edge_weight1, L0_gnn_eps, L0_gnn_We, L0_gnn_be, L0_gnn_W1, L0_gnn_b1, L0_gnn_gamma, L0_gnn_beta, L0_gnn_W2, L0_gnn_b2), axis=-1)
    return x

_drawn_inputs = setup_inputs


def setup_inputs(seed=0):
    import zlib

    import numpy as np

    out = dict(_drawn_inputs(seed))
    spreads = {'L0_gnn_eps': (0.0, 2.0),
     'L0_gnn_be': (0.0, 0.1),
     'L0_gnn_b1': (0.0, 2.0),
     'L0_gnn_gamma': (1.0, 0.2),
     'L0_gnn_beta': (0.0, 0.1),
     'L0_gnn_b2': (0.0, 0.1)}
    factors = {}
    for name, (base, spread) in spreads.items():
        noise = np.random.default_rng([zlib.crc32(name.encode()), seed]).standard_normal(out[name].shape)
        drawn = base * np.exp(spread * noise) if base else spread * noise
        out[name] = jnp.asarray(drawn.astype(out[name].dtype))
    for name, factor in factors.items():
        out[name] = (out[name] * factor).astype(out[name].dtype)
    return out
```

```python
import concourse.bass as bass
from concourse import mybir
from contextlib import ExitStack



def gnn_layers(nc, x_pad, src_t, dst_t, w_t, We, be, W1, W2, b2, vectors, eps, out):
    fp32 = mybir.dt.float32
    i32 = mybir.dt.int32
    ALU = mybir.AluOpType
    ACT = mybir.ActivationFunctionType

    P = 128
    L, D, _ = W1.shape
    C = D // P
    N = out.shape[0]
    BLOCKS = x_pad.shape[0] // P
    T_PAD = src_t.shape[1]
    EDGES = 32 * N
    WIN, RUN, MARGIN = 64, 8, 16
    PAIR = 2 * RUN
    STEP = 2 * PAIR
    T = -(-EDGES // P)
    LAST = T - (BLOCKS - 1) * STEP
    assert T_PAD == BLOCKS * STEP and STEP * P == P * EDGES // N
    QUADS = STEP // 4
    EPS = 1e-05
    TAIL = N - (BLOCKS - 1) * P + MARGIN
    GUARD = 2 * P
    PLACED = WIN + 2 * MARGIN

    table = nc.dram_tensor("node_table", (N, D), fp32, kind="Internal").ap()

    def quads_of(runs):
        at, quads = 0, []
        for pair, tiles in enumerate(runs):
            for n in range(0, len(tiles), 4):
                quads.append([(4 * len(quads) + k, pair * PAIR + j, j // RUN)
                              for k, j in enumerate(tiles[n:n + 4])])
        return quads

    alternating = [k // 2 + RUN * (k % 2) for k in range(PAIR)]
    FULL = quads_of([alternating, alternating])
    short = [0, RUN] + list(range(1, RUN))
    assert LAST - PAIR == len(short) and FULL[3][0][0] == 12
    FINAL = quads_of([alternating, short])
    FQ = len(FINAL)

    ctx = ExitStack()
    with ctx:
        def sb(name, shape, dt=fp32):
            return ctx.enter_context(nc.sbuf_tensor(name, shape, dt))

        def sem(name):
            return ctx.enter_context(nc.semaphore(name))

        rows = sb("rows", [P, STEP, D])
        onehot = sb("onehot", [P, 2, PAIR, WIN])
        x_now = sb("x_now", [P, BLOCKS, D])
        x_in = sb("x_in", [P, BLOCKS, D])
        hT = sb("hT", [P, C, GUARD - MARGIN + BLOCKS * P])
        W1_sb = sb("W1_sb", [P, C, D])
        W2_sb = sb("W2_sb", [P, C, D])
        b2_bc = sb("b2_bc", [P, D])
        be_bc = sb("be_bc", [P, D])
        We_bc = sb("We_bc", [P, D])
        pair_sb = sb("pair_sb", [P, 2, D])
        carry = sb("carry", [P, D])
        u = sb("u", [P, D])
        uT = sb("uT", [P, C, P])
        src_all = sb("src_all", [P, T_PAD], i32)
        dst_all = sb("dst_all", [P, T_PAD], i32)
        w_all = sb("w_all", [P, T_PAD])
        negw_all = sb("negw_all", [P, T_PAD])
        row_all = sb("row_all", [P, T_PAD])
        local_all = sb("local_all", [P, T_PAD])
        starts = sb("starts", [P, T_PAD])
        outside = sb("outside", [P, T_PAD])
        src_cur = sb("src_cur", [P, STEP], i32)
        negw_cur = sb("negw_cur", [P, STEP])
        cols = sb("cols", [P, 2 * P])
        part = sb("part", [P, 1])
        upper = sb("upper", [P, 1])
        target = sb("target", [P, 1])
        ident = sb("ident", [P, P])
        place = sb("place", [P, 2 * P])
        ones = sb("ones", [P, P])
        node = sb("node", [P, BLOCKS])
        mask = sb("mask", [P, BLOCKS])
        mask_lo = sb("mask_lo", [P, BLOCKS])
        bad = sb("bad", [P, 1])
        ok = sb("ok", [P, 1])
        flag = sb("flag", [1, 1], i32)
        pair_w = sb("pair_w", [P, 2, BLOCKS + 1])
        w_sum = sb("w_sum", [P, BLOCKS])
        w_sum_cur = sb("w_sum_cur", [P, 1])
        vec = sb("vec", [P, 3, C])
        eps_cur = sb("eps_cur", [P, 1])
        eps1 = sb("eps1", [P, 1])
        stats = sb("stats", [P, C, BLOCKS + 1, 6])
        mv = sb("mv", [P, C, 2])
        eps_col = sb("eps_col", [P, 1])
        std = sb("std", [P, C])
        rstd = sb("rstd", [P, C])
        bn_scale = sb("bn_scale", [P, C])
        bn_shift = sb("bn_shift", [P, C])
        bn_bias = sb("bn_bias", [P, C])
        ln_stats = sb("ln_stats", [P, BLOCKS, 6])
        ln_mv = sb("ln_mv", [P, BLOCKS, 2])
        ln_std = sb("ln_std", [P, BLOCKS])
        ln_rstd = sb("ln_rstd", [P, BLOCKS])
        src_one = sb("src_one", [P, 1], i32)
        negw_one = sb("negw_one", [P, 1])
        row_one = sb("row_one", [P, 1])
        onehot_block = sb("onehot_block", [P, P])

        def pb(name, shape):
            return ctx.enter_context(nc.psum_tensor(name, shape, fp32))

        We_ps = pb("We_ps", [P, D])
        pair_ps = [pb(f"pair_ps{h}", [P, D]) for h in range(2)]
        uT_ps = pb("uT_ps", [P, C, P])
        h_ps = pb("h_ps", [P, C, P])
        y_ps = [pb(f"y_ps{b}", [P, D]) for b in range(3)]

        x_loaded = sem("x_loaded")
        tables_loaded = sem("tables_loaded")
        first_loaded = sem("first_loaded")
        iotas = sem("iotas")
        prep = sem("prep")
        masks_ready = sem("masks_ready")
        w_cols_ready = [sem(f"w_cols_ready{h}") for h in range(2)]
        w_onehot_ready = [sem(f"w_onehot_ready{h}") for h in range(2)]
        w_summed = [sem(f"w_summed{h}") for h in range(2)]
        w_copied = sem("w_copied")
        bad_counted = sem("bad_counted")
        w_placed = sem("w_placed")
        flag_ready = sem("flag_ready")
        We_ready = sem("We_ready")
        staged = sem("staged")
        table_written = sem("table_written")
        params_free = sem("params_free")
        params_loaded = sem("params_loaded")
        cols_ready = sem("cols_ready")
        landed = [sem(f"landed{q}") for q in range(QUADS)]
        v_ready = [sem(f"v_ready{q}") for q in range(QUADS)]
        quad_summed = [sem(f"quad_summed{q}") for q in range(QUADS)]
        onehot_ready = sem("onehot_ready")
        pair_copied = [sem(f"pair_copied{h}") for h in range(2)]
        carry_cleared = sem("carry_cleared")
        carry_copied = sem("carry_copied")
        eps_ready = sem("eps_ready")
        u_scaled = sem("u_scaled")
        u_ready = sem("u_ready")
        block_summed = sem("block_summed")
        uT_copied = sem("uT_copied")
        h_summed = sem("h_summed")
        h_copied = sem("h_copied")
        stats_done = sem("stats_done")
        var_ready = sem("var_ready")
        std_ready = sem("std_ready")
        ln_var_ready = sem("ln_var_ready")
        ln_std_ready = sem("ln_std_ready")
        bn_chain = sem("bn_chain")
        bn_ready = sem("bn_ready")
        hr_ready = sem("hr_ready")
        y_summed = sem("y_summed")
        y_added = sem("y_added")
        x_updated = sem("x_updated")
        ln_chain = sem("ln_chain")
        ln_scaled = sem("ln_scaled")
        ln_ready = sem("ln_ready")
        out_written = sem("out_written")
        slow_cols = sem("slow_cols")
        slow_landed = sem("slow_landed")
        slow_chain = sem("slow_chain")
        slow_onehot = sem("slow_onehot")
        slow_summed = sem("slow_summed")
        slow_done = sem("slow_done")
        slow_cleared = sem("slow_cleared")
        slow_u = sem("slow_u")
        waited = sem("waited")

        def y_stage(b):
            return rows[:, b, :]

        def table_stage(b):
            return rows[:, STEP // 2 + b, :]

        SLOW_SUMS = 8

        def real_rows(b):
            lo = MARGIN if b == 0 else 0
            hi = TAIL if b == BLOCKS - 1 else P
            cuts = [lo, hi] if hi % 16 == 0 else [lo, hi - hi % 16, hi]
            return [(a, z, b * P - MARGIN + a) for a, z in zip(cuts, cuts[1:])]

        WRITES = 16 * sum(len(real_rows(b)) for b in range(BLOCKS))
        PARAMS = 16 * 7

        def quad_count(q, l, i):
            return (BLOCKS if q < FQ else BLOCKS - 1) * l + i

        def landed_count(q, l, i):
            if q < FQ - 1:
                return 64 * (BLOCKS * l + i)
            if q == FQ - 1:
                return (64 * (BLOCKS - 1) + 16 * len(FINAL[-1])) * l + 64 * i
            return 64 * (BLOCKS - 1) * l + 64 * i

        def wait_alone(engine, semaphore, value):
            engine.wait_ge(semaphore, value)
            engine.sem_inc(waited, 1)

        block = ctx.enter_context(nc.Block())

        @block.sync
        def _(sp):
            sp.dma_start(dst_all[:, :], dst_t).then_inc(tables_loaded, 16)
            sp.dma_start(w_all[:, :], w_t).then_inc(tables_loaded, 16)
            sp.dma_start(src_all[:, :], src_t).then_inc(tables_loaded, 16)
            sp.dma_start(be_bc[:, :], be[0:1, :].to_broadcast([P, D])).then_inc(first_loaded, 16)
            sp.dma_start(We_bc[:, :], We[0:1, :].to_broadcast([P, D])).then_inc(first_loaded, 16)
            x_blocks = x_pad.rearrange("(b p) d -> p b d", p=P)
            sp.dma_start(x_in[:, :, :], x_blocks).then_inc(x_loaded, 16)
            sp.dma_start(x_now[:, :, :], x_blocks).then_inc(x_loaded, 16)

            def write_table(l):
                for b in range(BLOCKS):
                    sp.wait_ge(staged, BLOCKS * l + b + 1)
                    for a, z, n in real_rows(b):
                        sp.dma_start(table[n:n + z - a, :], rows[a:z, STEP // 2 + b, :]).then_inc(table_written, 16)

            write_table(0)
            with sp.Fori(0, L) as l:
                wait_alone(sp, params_free, 3 * l + 3)
                sp.dma_start(eps_cur[:, :], eps[bass.ds(l, 1), :].to_broadcast([P, 1])).then_inc(params_loaded, 16)
                sp.dma_start(vec[:, :, :], vectors[bass.ds(l, 1), :, :, :].rearrange("o p v c -> p (o v) c")).then_inc(params_loaded, 16)
                sp.dma_start(W1_sb[:, :, :], W1[bass.ds(l, 1), :, :].rearrange("o (c p) d -> p (o c) d", p=P)).then_inc(params_loaded, 16)
                sp.dma_start(W2_sb[:, :, :], W2[bass.ds(l, 1), :, :].rearrange("o (c p) d -> p (o c) d", p=P)).then_inc(params_loaded, 16)
                sp.dma_start(b2_bc[:, :], b2[bass.ds(l, 1), :].to_broadcast([P, D])).then_inc(params_loaded, 16)
                sp.dma_start(be_bc[:, :], be[bass.ds(l + 1, 1), :].to_broadcast([P, D])).then_inc(params_loaded, 16)
                sp.dma_start(We_bc[:, :], We[bass.ds(l + 1, 1), :].to_broadcast([P, D])).then_inc(params_loaded, 16)
                write_table(l + 1)
            for b in range(BLOCKS):
                sp.wait_ge(ln_ready, b + 1)
                for a, z, n in real_rows(b):
                    sp.dma_start(out[n:n + z - a, :], rows[a:z, b, :]).then_inc(out_written, 16)
            sp.wait_ge(table_written, (L + 1) * WRITES)
            sp.wait_ge(out_written, WRITES)

        @block.gpsimd
        def _(pool):
            nc.gpsimd.iota(cols[:, :], [[1, 2 * P]], base=0, channel_multiplier=0,
                           allow_small_or_imprecise_dtypes=True)
            nc.gpsimd.iota(part[:, :], [[0, 1]], base=0, channel_multiplier=1,
                           allow_small_or_imprecise_dtypes=True)
            nc.gpsimd.iota(node[:, :], [[P, BLOCKS]], base=-MARGIN, channel_multiplier=1,
                           allow_small_or_imprecise_dtypes=True)
            nc.gpsimd.iota(starts[:, :], [[WIN // 2, T_PAD // RUN], [0, RUN]], base=0, channel_multiplier=0,
                           allow_small_or_imprecise_dtypes=True).then_inc(iotas, 1)

            def gather(quads, l, i):
                for q, quad in enumerate(quads):
                    if q % 4 == 0:
                        pool.wait_ge(cols_ready, 2 * BLOCKS * l + 2 * i + q // 4 + 1)
                    wait_alone(pool, quad_summed[q], quad_count(q, l, i) + 1)
                    for slot, tile, _ in quad:
                        nc.gpsimd.indirect_dma_start(
                            rows[:, slot, :], None, table[:, :],
                            bass.IndirectOffsetOnAxis(src_cur[:, tile:tile + 1], 0)).then_inc(landed[q], 16)

            pool.wait_ge(flag_ready, 1)
            slow = pool.value_load(flag[0:1, 0:1], min_val=0, max_val=1)
            with pool.Fori(0, L) as l:
                pool.wait_ge(table_written, WRITES * (l + 1))
                wait_alone(pool, x_updated, BLOCKS * l + 1)
                with pool.If(slow == 0):
                    with pool.Fori(0, BLOCKS - 1) as i:
                        gather(FULL, l, i)
                    gather(FINAL, l, BLOCKS - 1)
                with pool.Else():
                    with pool.Fori(0, T) as t:
                        wait_alone(pool, slow_cols, T * l + t + 1)
                        nc.gpsimd.indirect_dma_start(
                            rows[:, 0, :], None, table[:, :],
                            bass.IndirectOffsetOnAxis(src_one[:, 0:1], 0)).then_inc(slow_landed, 16)
                pool.nop()

        @block.scalar
        def _(act):
            act.wait_ge(masks_ready, 1)
            act.wait_ge(first_loaded, 32)
            nc.scalar.copy(We_ps[:, :], We_bc[:, :]).then_inc(We_ready, 1)
            with act.Fori(0, BLOCKS) as i:
                for h in range(2):
                    act.wait_ge(w_summed[h], i + 1)
                    nc.scalar.copy(negw_cur[:, h * PAIR:(h + 1) * PAIR],
                                   negw_all[:, bass.ds(STEP * i + h * PAIR, PAIR)]).then_inc(w_cols_ready[h], 1)
                for h in range(2):
                    act.wait_ge(w_summed[h], i + 2)
                    nc.scalar.mul(pair_w[:, h, bass.ds(i + 1, 1)], y_ps[h][:, 0:1], -1.0).then_inc(w_copied, 1)
            act.wait_ge(x_loaded, 32)

            def move_cols(step, h):
                nc.scalar.copy(src_cur[:, h * PAIR:(h + 1) * PAIR], src_all[:, bass.ds(STEP * step + h * PAIR, PAIR)])
                nc.scalar.copy(negw_cur[:, h * PAIR:(h + 1) * PAIR],
                               negw_all[:, bass.ds(STEP * step + h * PAIR, PAIR)]).then_inc(cols_ready, 1)

            def scale_u(n, i):
                act.wait_ge(block_summed, n + 1)
                nc.scalar.copy(w_sum_cur[:, :], w_sum[:, bass.ds(i, 1)])
                nc.scalar.activation(u[:, :], x_now[:, bass.ds(i, 1), :].rearrange("p o d -> p (o d)"),
                                     ACT.Identity, scale=eps1[:, 0:1]).then_inc(u_scaled, 1)

            def copy_pair(h, n, summed, value):
                act.wait_ge(block_summed, n + 1)
                act.wait_ge(summed, value)
                nc.scalar.copy(pair_sb[:, h, :], pair_ps[h][:, :]).then_inc(pair_copied[h], 1)

            def finish_block(n, i):
                act.wait_ge(block_summed, n + 2)
                act.wait_ge(h_summed, n + 1)
                nc.scalar.copy(uT[:, :, :], uT_ps[:, :, :]).then_inc(uT_copied, 1)

            def finish_h(n, i):
                act.wait_ge(h_summed, n + 2)
                for c in range(C):
                    last = nc.scalar.activation(
                        hT[:, c:c + 1, bass.ds(P * i + GUARD - MARGIN, P)].rearrange("p o n -> p (o n)"),
                        h_ps[:, c, :], ACT.Identity, bias=vec[:, 0, c:c + 1])
                last.then_inc(h_copied, 1)

            act.wait_ge(flag_ready, 1)
            slow = act.value_load(flag[0:1, 0:1], min_val=0, max_val=1)
            with act.Fori(0, L) as l:
                act.wait_ge(params_loaded, PARAMS * (l + 1))
                nc.scalar.activation(eps1[:, :], eps_cur[:, :], ACT.Identity, bias=1.0).then_inc(eps_ready, 1)
                wait_alone(act, eps_ready, l + 1)
                with act.If(slow == 0):
                    move_cols(0, 0)
                    move_cols(0, 1)
                    with act.Fori(0, BLOCKS - 1) as i:
                        n = BLOCKS * l + i
                        scale_u(n, i)
                        act.wait_ge(v_ready[3], quad_count(3, l, i) + 1)
                        move_cols(i + 1, 0)
                        copy_pair(0, n, quad_summed[3], quad_count(3, l, i) + 2)
                        act.wait_ge(v_ready[7], quad_count(7, l, i) + 1)
                        move_cols(i + 1, 1)
                        copy_pair(1, n, quad_summed[7], quad_count(7, l, i) + 2)
                        finish_block(n, i)
                        nc.scalar.copy(carry[3 * P // 4:P, :], pair_sb[3 * P // 4:P, 1, :]).then_inc(carry_copied, 1)
                        finish_h(n, i)
                    i = BLOCKS - 1
                    n = BLOCKS * l + i
                    scale_u(n, i)
                    copy_pair(0, n, quad_summed[3], quad_count(3, l, i) + 2)
                    copy_pair(1, n, quad_summed[FQ - 1], quad_count(FQ - 1, l, i) + 2)
                    finish_block(n, i)
                    finish_h(n, i)
                with act.Else():
                    with act.Fori(0, T) as t:
                        act.wait_ge(slow_done, T * l + t + 1)
                        nc.scalar.copy(src_one[:, :], src_all[:, bass.ds(t, 1)])
                        nc.scalar.copy(row_one[:, :], row_all[:, bass.ds(t, 1)])
                        nc.scalar.copy(negw_one[:, :], negw_all[:, bass.ds(t, 1)]).then_inc(slow_cols, 1)
                    with act.Fori(0, BLOCKS) as i:
                        n = BLOCKS * l + i
                        scale_u(n, i)
                        finish_block(n, i)
                        finish_h(n, i)
                act.wait_ge(var_ready, l + 1)
                nc.scalar.activation(std[:, :], mv[:, :, 1], ACT.Sqrt, bias=eps_col[:, 0:1]).then_inc(std_ready, 1)
                act.wait_ge(bn_ready, l + 1)
                for b in range(BLOCKS):
                    at = GUARD - MARGIN + P * b
                    for c in range(C):
                        last = nc.scalar.activation(hT[:, c, at:at + P], hT[:, c, at:at + P], ACT.Relu,
                                                    bias=bn_bias[:, c:c + 1], scale=bn_scale[:, c:c + 1])
                    last.then_inc(hr_ready, 1)
                nc.scalar.copy(We_ps[:, :], We_bc[:, :]).then_inc(We_ready, 1)
                for b in range(BLOCKS):
                    act.wait_ge(y_added, BLOCKS * l + b + 1)
                    nc.scalar.activation(x_now[:, b, :], y_stage(b), ACT.Relu,
                                         scale=mask[:, b:b + 1]).then_inc(x_updated, 1)
                act.wait_ge(x_updated, BLOCKS * (l + 1) + 1)
                act.sem_inc(params_free, 1)
            for b in range(BLOCKS):
                act.wait_ge(ln_var_ready, b + 1)
                nc.scalar.activation(ln_std[:, b:b + 1], ln_mv[:, b, 1:2], ACT.Sqrt,
                                     bias=eps_col[:, 0:1]).then_inc(ln_std_ready, 1)

        @block.vector
        def _(dve):
            done = [0]

            def then_wait(ins):
                done[0] += 1
                ins.then_inc(prep, 1)
                dve.wait_ge(prep, done[0])

            nc.vector.memset(ones[:, :], 1.0)
            nc.vector.memset(eps_col[:, :], EPS)
            nc.vector.memset(hT[:, :, 0:GUARD], 0.0)
            nc.vector.memset(carry[:, :], 0.0)
            nc.vector.memset(pair_w[:, :, 0:1], 0.0)
            dve.wait_ge(tables_loaded, 48)
            nc.vector.tensor_scalar(row_all[:, :], dst_all[:, :], float(MARGIN), None, ALU.add)
            then_wait(nc.vector.tensor_scalar(negw_all[:, :], w_all[:, :], -1.0, None, ALU.mult))
            dve.wait_ge(iotas, 1)
            nc.vector.tensor_scalar(upper[:, :], part[:, :], float(WIN), -float(WIN - 2 * MARGIN), ALU.is_ge, ALU.mult)
            nc.vector.tensor_scalar(ident[:, :], cols[:, 0:P], part[:, 0:1], None, ALU.is_equal)
            nc.vector.tensor_scalar(mask_lo[:, :], node[:, :], 0.0, None, ALU.is_ge)
            then_wait(nc.vector.tensor_tensor(local_all[:, :], row_all[:, :], starts[:, :], ALU.subtract))
            then_wait(nc.vector.scalar_tensor_tensor(target[:, :], part[:, :], float(WIN), upper[:, :], ALU.add, ALU.add))
            nc.vector.tensor_scalar(place[:, :], cols[:, :], target[:, 0:1], None, ALU.is_equal)
            nc.vector.scalar_tensor_tensor(mask[:, :], node[:, :], float(N), mask_lo[:, :], ALU.is_lt, ALU.mult)
            then_wait(nc.vector.tensor_scalar(outside[:, :], local_all[:, :], 0.0, None, ALU.is_lt))
            nc.vector.scalar_tensor_tensor(outside[:, :], local_all[:, :], float(WIN - 1), outside[:, :],
                                           ALU.is_gt, ALU.add, accum_out=bad[:, :]).then_inc(bad_counted, 1)
            for s in w_summed + quad_summed + pair_copied + [w_copied, carry_copied, block_summed, uT_copied,
                                                             h_summed, h_copied, slow_done, x_updated]:
                dve.sem_inc(s, 1)
            dve.sem_inc(masks_ready, 1)
            dve.wait_ge(x_loaded, 32)
            dve.wait_ge(first_loaded, 32)
            for b in range(BLOCKS):
                nc.vector.tensor_tensor(table_stage(b), x_in[:, b, :], be_bc[:, :], ALU.add).then_inc(staged, 1)

            def make_onehot(i, h, ready):
                nc.vector.tensor_tensor(
                    onehot[:, h, :, :], cols[:, 0:WIN].unsqueeze(1).to_broadcast([P, PAIR, WIN]),
                    local_all[:, bass.ds(STEP * i + h * PAIR, PAIR)].unsqueeze(2).to_broadcast([P, PAIR, WIN]),
                    ALU.is_equal).then_inc(ready, 1)

            with dve.Fori(0, BLOCKS) as i:
                for h in range(2):
                    dve.wait_ge(w_summed[h], i + 1)
                    make_onehot(i, h, w_onehot_ready[h])
            dve.wait_ge(w_placed, 1)
            then_wait(nc.vector.tensor_scalar(ok[:, :], y_ps[2][:, BLOCKS:BLOCKS + 1], 0.0, None, ALU.is_equal))
            nc.vector.tensor_scalar(w_sum[:, :], y_ps[2][:, 0:BLOCKS], ok[:, 0:1], None, ALU.mult)
            nc.vector.tensor_scalar(flag[:, :], ok[0:1, 0:1], 0.0, None, ALU.is_equal).then_inc(flag_ready, 1)
            dve.sem_inc(params_free, 3)

            def messages(quads, q, l, i):
                quad = quads[q]
                dve.wait_ge(landed[q], landed_count(q, l, i) + 16 * len(quad))
                for slot, tile, _ in quad:
                    last = nc.vector.scalar_tensor_tensor(rows[:, slot, :], We_ps[:, :], negw_cur[:, tile:tile + 1],
                                                          rows[:, slot, :], ALU.mult, ALU.max)
                last.then_inc(v_ready[q], 1)

            def finish_u(n, ready):
                dve.wait_ge(u_scaled, n + 1)
                return nc.vector.scalar_tensor_tensor(u[:, :], We_ps[:, :], w_sum_cur[:, 0:1], u[:, :],
                                                      ALU.mult, ALU.add).then_inc(ready, 1)

            def block_stats(n, i):
                dve.wait_ge(h_copied, n + 1)
                for c in range(C):
                    last = nc.vector.bn_stats(stats[:, c, bass.ds(i, 1), :].rearrange("p o s -> p (o s)"),
                                              hT[:, c:c + 1, bass.ds(P * i, P)].rearrange("p o n -> p (o n)"))
                return last

            def edge_step(quads, l, i):
                n = BLOCKS * l + i
                for h in range(2):
                    for q in ([3] if h == 0 else [FQ - 1, 7]):
                        dve.wait_ge(quad_summed[q], quad_count(q, l, i) + 1)
                    make_onehot(i, h, onehot_ready)
                    dve.wait_ge(cols_ready, 2 * BLOCKS * l + 2 * i + h + 1)
                    for q in range(4 * h, min(4 * h + 4, len(quads))):
                        messages(quads, q, l, i)
                        if q == 2:
                            finish_u(n, u_ready)
                        if q == 5:
                            block_stats(n, i)

            dve.wait_ge(flag_ready, 1)
            slow = dve.value_load(flag[0:1, 0:1], min_val=0, max_val=1)
            with dve.Fori(0, L) as l:
                dve.wait_ge(x_updated, BLOCKS * l + 1)
                nc.vector.memset(carry[3 * P // 4:P, :], 0.0).then_inc(carry_cleared, 1)
                wait_alone(dve, We_ready, l + 1)
                with dve.If(slow == 0):
                    with dve.Fori(0, BLOCKS - 1) as i:
                        edge_step(FULL, l, i)
                    edge_step(FINAL, l, BLOCKS - 1)
                with dve.Else():
                    sums = rows[:, SLOW_SUMS:SLOW_SUMS + BLOCKS, :]
                    nc.vector.memset(sums, 0.0).then_inc(slow_cleared, 1)
                    wait_alone(dve, slow_cleared, l + 1)
                    with dve.Fori(0, T) as t:
                        k0 = (2 + BLOCKS) * (T * l + t)
                        dve.wait_ge(slow_landed, 16 * (T * l + t + 1))
                        nc.vector.scalar_tensor_tensor(rows[:, 0, :], We_ps[:, :], negw_one[:, 0:1], rows[:, 0, :],
                                                       ALU.mult, ALU.max).then_inc(slow_chain, 1)
                        dve.wait_ge(slow_chain, k0 + 1)
                        nc.vector.scalar_tensor_tensor(rows[:, 1, :], We_ps[:, :], negw_one[:, 0:1], rows[:, 0, :],
                                                       ALU.mult, ALU.subtract).then_inc(slow_chain, 1)
                        for b in range(BLOCKS):
                            m = BLOCKS * (T * l + t) + b
                            dve.wait_ge(slow_chain, k0 + 2 + b)
                            nc.vector.tensor_scalar(onehot_block[:, :], cols[:, 0:P], float(P * b), row_one[:, 0:1],
                                                    ALU.add, ALU.is_equal).then_inc(slow_onehot, 1)
                            dve.wait_ge(slow_summed, m + 1)
                            nc.vector.tensor_tensor(sums[:, b, :], sums[:, b, :], y_ps[0][:, :],
                                                    ALU.subtract).then_inc(slow_chain, 1)
                        dve.wait_ge(slow_chain, k0 + 2 + BLOCKS)
                        dve.sem_inc(slow_done, 1)
                    with dve.Fori(0, BLOCKS) as i:
                        n = BLOCKS * l + i
                        finish_u(n, slow_u)
                        dve.wait_ge(slow_u, n + 1)
                        nc.vector.tensor_tensor(
                            u[:, :], rows[:, bass.ds(SLOW_SUMS + i, 1), :].rearrange("p o d -> p (o d)"), u[:, :],
                            ALU.add).then_inc(u_ready, 1)
                        block_stats(n, i)
                dve.wait_ge(h_copied, BLOCKS * l + BLOCKS + 1)
                for c in range(C):
                    last = nc.vector.bn_stats(stats[:, c, BLOCKS, :], hT[:, c, GUARD + (BLOCKS - 2) * P:GUARD + N])
                last.then_inc(stats_done, 1)
                wait_alone(dve, stats_done, l + 1)
                for c in range(C):
                    last = nc.vector.bn_aggr(mv[:, c, :], stats[:, c, 2:BLOCKS + 1, :].rearrange("p s k -> p (s k)"))
                last.then_inc(var_ready, 1)
                dve.wait_ge(std_ready, l + 1)
                nc.vector.reciprocal(rstd[:, :], std[:, :]).then_inc(bn_chain, 1)
                dve.wait_ge(bn_chain, 3 * l + 1)
                dve.wait_ge(params_loaded, PARAMS * (l + 1))
                nc.vector.tensor_tensor(bn_scale[:, :], rstd[:, :], vec[:, 1, :], ALU.mult).then_inc(bn_chain, 1)
                dve.wait_ge(bn_chain, 3 * l + 2)
                nc.vector.tensor_tensor(bn_shift[:, :], mv[:, :, 0], bn_scale[:, :], ALU.mult).then_inc(bn_chain, 1)
                dve.wait_ge(bn_chain, 3 * l + 3)
                nc.vector.tensor_tensor(bn_bias[:, :], vec[:, 2, :], bn_shift[:, :], ALU.subtract).then_inc(bn_ready, 1)
                for b in range(BLOCKS):
                    dve.wait_ge(y_summed, BLOCKS * l + b + 1)
                    nc.vector.tensor_tensor(y_stage(b), y_ps[b % 3][:, :], b2_bc[:, :], ALU.add).then_inc(y_added, 1)
                    dve.wait_ge(y_added, BLOCKS * l + b + 1)
                    nc.vector.scalar_tensor_tensor(table_stage(b), y_stage(b), 0.0, be_bc[:, :],
                                                   ALU.max, ALU.add).then_inc(staged, 1)
                dve.wait_ge(staged, BLOCKS * (l + 2))
                dve.sem_inc(params_free, 1)
            dve.wait_ge(x_updated, BLOCKS * L + 1)
            dve.wait_ge(table_written, (L + 1) * WRITES)

            def ln_first(b):
                nc.vector.tensor_tensor(table_stage(b), x_in[:, b, :], x_now[:, b, :], ALU.add).then_inc(ln_chain, 1)
                dve.wait_ge(ln_chain, 2 * b + 1)
                nc.vector.bn_stats(ln_stats[:, b, :], table_stage(b)).then_inc(ln_chain, 1)
                dve.wait_ge(ln_chain, 2 * b + 2)
                nc.vector.bn_aggr(ln_mv[:, b, :], ln_stats[:, b, :]).then_inc(ln_var_ready, 1)

            def ln_second(b):
                dve.wait_ge(ln_std_ready, b + 1)
                nc.vector.reciprocal(ln_rstd[:, b:b + 1], ln_std[:, b:b + 1]).then_inc(ln_scaled, 1)
                dve.wait_ge(ln_scaled, b + 1)
                nc.vector.tensor_scalar(rows[:, b, :], table_stage(b), ln_mv[:, b, 0:1], ln_rstd[:, b:b + 1],
                                        ALU.subtract, ALU.mult).then_inc(ln_ready, 1)

            for b in range(BLOCKS):
                ln_first(b)
                if b:
                    ln_second(b - 1)
            ln_second(BLOCKS - 1)

        @block.tensor
        def _(pe):
            with pe.Fori(0, BLOCKS) as i:
                for h in range(2):
                    pe.wait_ge(w_onehot_ready[h], i + 1)
                    pe.wait_ge(w_cols_ready[h], i + 1)
                    pe.wait_ge(w_copied, 2 * i + 1)
                    for k in range(PAIR):
                        j, win = k // 2 + RUN * (k % 2), k % 2
                        last = nc.tensor.matmul(y_ps[h][WIN * win:WIN * (win + 1), 0:1], onehot[:, h, j, :],
                                                negw_cur[:, h * PAIR + j:h * PAIR + j + 1],
                                                start=(k < 2), stop=(k >= PAIR - 2))
                    last.then_inc(w_summed[h], 1)
            pe.wait_ge(bad_counted, 1)
            nc.tensor.matmul(y_ps[2][:, BLOCKS:BLOCKS + 1], ones[:, :], bad[:, :],
                             start=True, stop=True)
            pe.wait_ge(w_copied, 2 * BLOCKS + 1)
            nc.tensor.matmul(y_ps[2][:, 0:BLOCKS], place[:, WIN:WIN + P], pair_w[:, 0, 1:BLOCKS + 1],
                             start=True, stop=False)
            nc.tensor.matmul(y_ps[2][:, 0:BLOCKS], place[:, 0:P], pair_w[:, 1, 1:BLOCKS + 1],
                             start=False, stop=False)
            nc.tensor.matmul(y_ps[2][:, 0:BLOCKS], place[:, P:2 * P], pair_w[:, 1, 0:BLOCKS],
                             start=False, stop=True).then_inc(w_placed, 1)

            def sum_pair(quads, h, l, i):
                pe.wait_ge(pair_copied[h], BLOCKS * l + i + 1)
                pe.wait_ge(onehot_ready, 2 * BLOCKS * l + 2 * i + h + 1)
                tiles = [t for q in quads[4 * h:4 * h + 4] for t in q]
                firsts = {win: next(t for t in tiles if t[2] == win) for win in (0, 1)}
                lasts = {win: [t for t in tiles if t[2] == win][-1] for win in (0, 1)}
                for q in range(4 * h, min(4 * h + 4, len(quads))):
                    pe.wait_ge(v_ready[q], quad_count(q, l, i) + 1)
                    for t in quads[q]:
                        slot, tile, win = t
                        last = nc.tensor.matmul(pair_ps[h][WIN * win:WIN * (win + 1), :],
                                                onehot[:, h, tile - h * PAIR, :], rows[:, slot, :],
                                                start=(t == firsts[win]), stop=(t == lasts[win]))
                    last.then_inc(quad_summed[q], 1)

            def sum_block(n, l, i, pairs):
                pe.wait_ge(u_ready, n + 1)
                pe.wait_ge(uT_copied, n + 1)
                if pairs:
                    pe.wait_ge(carry_cleared, l + 1)
                    pe.wait_ge(carry_copied, (BLOCKS - 1) * l + i + 1)
                    pe.wait_ge(pair_copied[0], n + 2)
                    pe.wait_ge(pair_copied[1], n + 2)
                for c in range(C):
                    f = slice(c * P, (c + 1) * P)
                    last = nc.tensor.matmul(uT_ps[:, c, :], u[:, f], ident[:, :], start=True, stop=not pairs)
                    if pairs:
                        nc.tensor.matmul(uT_ps[:, c, 0:PLACED], pair_sb[:, 0, f], place[:, WIN:WIN + PLACED],
                                         start=False, stop=False)
                        nc.tensor.matmul(uT_ps[:, c, WIN:P], pair_sb[:, 1, f], place[:, WIN:P],
                                         start=False, stop=False)
                        last = nc.tensor.matmul(uT_ps[:, c, 0:PLACED - WIN], carry[:, f], place[:, P:WIN + PLACED],
                                                start=False, stop=True)
                last.then_inc(block_summed, 1)
                pe.wait_ge(uT_copied, n + 2)
                pe.wait_ge(h_copied, n + 1)
                for c in range(C):
                    for k in range(C):
                        last = nc.tensor.matmul(h_ps[:, c, :], W1_sb[:, k, c * P:(c + 1) * P], uT[:, k, :],
                                                start=(k == 0), stop=(k == C - 1))
                last.then_inc(h_summed, 1)

            pe.wait_ge(flag_ready, 1)
            slow = pe.value_load(flag[0:1, 0:1], min_val=0, max_val=1)
            with pe.Fori(0, L) as l:
                pe.wait_ge(params_loaded, PARAMS * (l + 1))
                with pe.If(slow == 0):
                    with pe.Fori(0, BLOCKS - 1) as i:
                        sum_pair(FULL, 0, l, i)
                        sum_pair(FULL, 1, l, i)
                        sum_block(BLOCKS * l + i, l, i, True)
                    i = BLOCKS - 1
                    sum_pair(FINAL, 0, l, i)
                    sum_pair(FINAL, 1, l, i)
                    sum_block(BLOCKS * l + i, l, i, True)
                with pe.Else():
                    with pe.Fori(0, T) as t:
                        for b in range(BLOCKS):
                            pe.wait_ge(slow_onehot, BLOCKS * (T * l + t) + b + 1)
                            nc.tensor.matmul(y_ps[0][:, :], onehot_block[:, :], rows[:, 1, :],
                                             start=True, stop=True).then_inc(slow_summed, 1)
                    with pe.Fori(0, BLOCKS) as i:
                        sum_block(BLOCKS * l + i, l, i, False)
                for b in range(BLOCKS):
                    pe.wait_ge(hr_ready, BLOCKS * l + b + 1)
                    if b >= 3:
                        pe.wait_ge(y_added, BLOCKS * l + b - 2)
                    at = GUARD - MARGIN + P * b
                    for c in range(C):
                        last = nc.tensor.matmul(y_ps[b % 3][:, :], hT[:, c, at:at + P], W2_sb[:, c, :],
                                                start=(c == 0), stop=(c == C - 1))
                    last.then_inc(y_summed, 1)
                pe.wait_ge(y_summed, BLOCKS * (l + 1))
                pe.sem_inc(params_free, 1)


def kernel(**inputs):
    import numpy as np
    import concourse.bacc as bacc
    from concourse.bass_utils import run_bass_kernel_spmd

    P, STEP, MARGIN = 128, 32, 16
    x = np.asarray(inputs["x"])
    N, D = x.shape
    src, dst, w = (np.asarray(inputs[k]).reshape(-1) for k in ("src", "dst", "edge_weight1"))
    blocks = -(-(N + MARGIN) // P)
    edges = blocks * STEP * P

    def padded(a, size, fill, before=0):
        out = np.full((size,) + a.shape[1:], fill, a.dtype)
        out[before:before + a.shape[0]] = a
        return out

    def by_tile(a, fill):
        return np.ascontiguousarray(padded(a, edges, fill).reshape(-1, P).T)

    We, be, W1, b1, gamma, beta, W2, b2, eps = (
        np.asarray(inputs["L0_gnn_" + k]) for k in ("We", "be", "W1", "b1", "gamma", "beta", "W2", "b2", "eps"))
    L = W1.shape[0]
    vectors = np.stack([v.reshape(L, D // P, P).transpose(0, 2, 1) for v in (b1, gamma, beta)], axis=2)
    arrays = {
        "x_pad": padded(x, blocks * P, 0, before=MARGIN),
        "src_t": by_tile(src, 0),
        "dst_t": by_tile(dst, N),
        "w_t": by_tile(w, 0),
        "We": padded(We.reshape(L, D), L + 1, 0),
        "be": padded(be, L + 1, 0),
        "W1": W1, "W2": W2, "b2": b2,
        "vectors": np.ascontiguousarray(vectors),
        "eps": eps.reshape(L, 1),
    }
    nc = bacc.Bacc("TRN2", target_bir_lowering=False, num_devices=1)
    args = [nc.dram_tensor(name, a.shape, mybir.dt.from_np(a.dtype), kind="ExternalInput").ap()
            for name, a in arrays.items()]
    out = nc.dram_tensor("out", (N, D), mybir.dt.float32, kind="ExternalOutput").ap()
    gnn_layers(nc, *args, out)
    result = run_bass_kernel_spmd(nc, [arrays], core_ids=[0])
    return result.results[0]["out"]
```

```python
import concourse.bass as bass
from concourse import mybir
from contextlib import ExitStack



def gnn_layers(nc, x_pad, src_t, dst_t, w_t, We, be, W1, W2, b2, vectors, eps, out):
    fp32 = mybir.dt.float32
    bf16 = mybir.dt.bfloat16
    i32 = mybir.dt.int32
    ALU = mybir.AluOpType
    ACT = mybir.ActivationFunctionType

    P = 128
    L, D, _ = W1.shape
    C = D // P
    N = out.shape[0]
    BLOCKS = x_pad.shape[0] // P
    T_PAD = src_t.shape[1]
    EDGES = 32 * N
    WIN, RUN, MARGIN = 64, 8, 16
    PAIR = 2 * RUN
    STEP = 2 * PAIR
    T = -(-EDGES // P)
    LAST = T - (BLOCKS - 1) * STEP
    assert T_PAD == BLOCKS * STEP and STEP * P == P * EDGES // N
    QUADS = STEP // 4
    EPS = 1e-05
    TAIL = N - (BLOCKS - 1) * P + MARGIN
    GUARD = 2 * P
    PLACED = WIN + 2 * MARGIN

    table = nc.dram_tensor("node_table", (N, D), fp32, kind="Internal").ap()

    def quads_of(pairs, last_split=RUN):
        quads = []
        for pair, (tiles, split) in enumerate(zip(pairs, (RUN, last_split))):
            for n in range(0, len(tiles), 4):
                quads.append([(4 * len(quads) + k, pair * PAIR + j, int(j >= split))
                              for k, j in enumerate(tiles[n:n + 4])])
        return quads

    alternating = [k // 2 + RUN * (k % 2) for k in range(PAIR)]
    FULL = quads_of([alternating, alternating])
    SHORT = LAST - PAIR
    SPLIT = (SHORT + 1) // 2
    short = [k // 2 + SPLIT * (k % 2) for k in range(SHORT)]
    FINAL = quads_of([alternating, short], SPLIT)
    FQ = len(FINAL)

    def tiles_of(quads, h):
        tiles = [t for q in quads[4 * h:4 * h + 4] for t in q]
        windows = [[t for t in tiles if t[2] == win] for win in (0, 1)]
        return tiles, [w[0] for w in windows], [w[-1] for w in windows]

    ctx = ExitStack()
    with ctx:
        def sb(name, shape, dt=fp32):
            return ctx.enter_context(nc.sbuf_tensor(name, shape, dt))

        def sem(name):
            return ctx.enter_context(nc.semaphore(name))

        rows = sb("rows", [P, STEP, D])
        onehot = sb("onehot", [P, 2, PAIR, WIN])
        x_now = sb("x_now", [P, BLOCKS, D])
        x_in = sb("x_in", [P, BLOCKS, D])
        hT = sb("hT", [P, C, GUARD - MARGIN + BLOCKS * P])
        W1_sb = sb("W1_sb", [P, C, D])
        W2_sb = sb("W2_sb", [P, C, D])
        b2_bc = sb("b2_bc", [P, D])
        be_bc = sb("be_bc", [P, D])
        We_bc = sb("We_bc", [P, D])
        pair_sb = sb("pair_sb", [P, 2, D])
        carry = sb("carry", [P, D])
        u = sb("u", [P, D])
        uT = sb("uT", [P, C, P])
        src_all = sb("src_all", [P, T_PAD], i32)
        dst_all = sb("dst_all", [P, T_PAD], i32)
        w_all = sb("w_all", [P, T_PAD])
        rest = sb("rest", [P, T_PAD])
        w_parts = sb("w_parts", [P, T_PAD + STEP, 3], bf16)
        w_parts_cur = sb("w_parts_cur", [P, STEP, 3], bf16)
        onehot_bf = sb("onehot_bf", [P, 2, PAIR, WIN], bf16)
        negw_all = sb("negw_all", [P, T_PAD])
        row_all = sb("row_all", [P, T_PAD])
        local_all = sb("local_all", [P, T_PAD])
        starts = sb("starts", [P, T_PAD])
        outside = sb("outside", [P, T_PAD])
        src_cur = sb("src_cur", [P, STEP], i32)
        negw_cur = sb("negw_cur", [P, STEP])
        cols = sb("cols", [P, 2 * P])
        part = sb("part", [P, 1])
        upper = sb("upper", [P, 1])
        target = sb("target", [P, 1])
        ident = sb("ident", [P, P])
        place = sb("place", [P, 2 * P])
        ones = sb("ones", [P, P])
        node = sb("node", [P, BLOCKS])
        mask = sb("mask", [P, BLOCKS])
        mask_lo = sb("mask_lo", [P, BLOCKS])
        bad = sb("bad", [P, 1])
        ok = sb("ok", [P, 1])
        flag = sb("flag", [1, 1], i32)
        pair_w = sb("pair_w", [P, 2, BLOCKS + 1, 3])
        w_sum = sb("w_sum", [P, BLOCKS])
        w_sum_cur = sb("w_sum_cur", [P, 1])
        vec = sb("vec", [P, 3, C])
        eps_cur = sb("eps_cur", [P, 1])
        eps1 = sb("eps1", [P, 1])
        stats = sb("stats", [P, C, BLOCKS + 2, 6])
        mv = sb("mv", [P, C, 2])
        eps_col = sb("eps_col", [P, 1])
        std = sb("std", [P, C])
        rstd = sb("rstd", [P, C])
        bn_scale = sb("bn_scale", [P, C])
        bn_shift = sb("bn_shift", [P, C])
        bn_bias = sb("bn_bias", [P, C])
        ln_stats = sb("ln_stats", [P, BLOCKS, 6])
        ln_mv = sb("ln_mv", [P, BLOCKS, 2])
        ln_std = sb("ln_std", [P, BLOCKS])
        ln_rstd = sb("ln_rstd", [P, BLOCKS])
        src_one = sb("src_one", [P, 1], i32)
        negw_one = sb("negw_one", [P, 1])
        row_one = sb("row_one", [P, 1])
        onehot_block = sb("onehot_block", [P, P])

        def pb(name, shape):
            return ctx.enter_context(nc.psum_tensor(name, shape, fp32))

        We_ps = pb("We_ps", [P, D])
        pair_ps = [pb(f"pair_ps{h}", [P, D]) for h in range(2)]
        uT_ps = pb("uT_ps", [P, C, P])
        h_ps = pb("h_ps", [P, C, P])
        y_ps = [pb(f"y_ps{b}", [P, D]) for b in range(3)]

        x_loaded = [sem(f"x_loaded{k}") for k in range(BLOCKS // 2)]
        dst_loaded = sem("dst_loaded")
        w_loaded = sem("w_loaded")
        src_loaded = sem("src_loaded")
        be_loaded = sem("be_loaded")
        We_loaded = sem("We_loaded")
        iotas = sem("iotas")
        cleared = sem("cleared")
        prep = sem("prep")
        masks_ready = sem("masks_ready")
        w_cols_ready = [sem(f"w_cols_ready{h}") for h in range(2)]
        w_onehot_ready = [sem(f"w_onehot_ready{h}") for h in range(2)]
        w_summed = [sem(f"w_summed{h}") for h in range(2)]
        w_cleared = sem("w_cleared")
        w_parts_ready = sem("w_parts_ready")
        w_copied = sem("w_copied")
        bad_counted = sem("bad_counted")
        bad_summed = sem("bad_summed")
        w_placed = sem("w_placed")
        w_sum_ready = sem("w_sum_ready")
        x_copied = sem("x_copied")
        flag_ready = sem("flag_ready")
        We_ready = sem("We_ready")
        staged = sem("staged")
        table_written = sem("table_written")
        params_free = sem("params_free")
        params_loaded = sem("params_loaded")
        cols_ready = sem("cols_ready")
        landed = [sem(f"landed{q}") for q in range(QUADS)]
        v_ready = [sem(f"v_ready{q}") for q in range(QUADS)]
        quad_summed = [sem(f"quad_summed{q}") for q in range(QUADS)]
        onehot_ready = sem("onehot_ready")
        pair_copied = [sem(f"pair_copied{h}") for h in range(2)]
        carry_cleared = sem("carry_cleared")
        carry_copied = sem("carry_copied")
        eps_ready = sem("eps_ready")
        u_scaled = sem("u_scaled")
        u_ready = sem("u_ready")
        block_summed = sem("block_summed")
        uT_copied = sem("uT_copied")
        h_summed = sem("h_summed")
        h_copied = sem("h_copied")
        h_part_summed = sem("h_part_summed")
        h_part_copied = sem("h_part_copied")
        stats_done = sem("stats_done")
        var_ready = sem("var_ready")
        std_ready = sem("std_ready")
        ln_var_ready = sem("ln_var_ready")
        ln_std_ready = sem("ln_std_ready")
        bn_chain = sem("bn_chain")
        bn_ready = sem("bn_ready")
        hr_ready = sem("hr_ready")
        y_summed = sem("y_summed")
        y_added = sem("y_added")
        x_updated = sem("x_updated")
        ln_chain = sem("ln_chain")
        ln_scaled = sem("ln_scaled")
        ln_ready = sem("ln_ready")
        out_written = sem("out_written")
        slow_cols = sem("slow_cols")
        slow_landed = sem("slow_landed")
        slow_chain = sem("slow_chain")
        slow_onehot = sem("slow_onehot")
        slow_summed = sem("slow_summed")
        slow_done = sem("slow_done")
        slow_cleared = sem("slow_cleared")
        slow_u = sem("slow_u")
        waited = sem("waited")

        def y_stage(b):
            return rows[:, b, :]

        def table_stage(b):
            return rows[:, STEP // 2 + b, :]

        def last_h(c):
            return h_ps[:, 0, :] if c == 0 else y_ps[c - 1][:, 0:P]

        SLOW_SUMS = 8

        def real_rows(b):
            lo = MARGIN if b == 0 else 0
            hi = TAIL if b == BLOCKS - 1 else P
            cuts = [lo, hi] if hi % 16 == 0 else [lo, hi - hi % 16, hi]
            return [(a, z, b * P - MARGIN + a) for a, z in zip(cuts, cuts[1:])]

        WRITES = 16 * sum(len(real_rows(b)) for b in range(BLOCKS))
        PARAMS = 16 * 7

        def quad_count(q, l, i):
            return (BLOCKS if q < FQ else BLOCKS - 1) * l + i

        def landed_count(q, l, i):
            if q < FQ - 1:
                return 64 * (BLOCKS * l + i)
            if q == FQ - 1:
                return (64 * (BLOCKS - 1) + 16 * len(FINAL[-1])) * l + 64 * i
            return 64 * (BLOCKS - 1) * l + 64 * i

        def wait_alone(engine, semaphore, value):
            engine.wait_ge(semaphore, value)
            engine.sem_inc(waited, 1)

        block = ctx.enter_context(nc.Block())

        @block.sync
        def _(sp):
            sp.dma_start(dst_all[:, :], dst_t).then_inc(dst_loaded, 16)
            sp.dma_start(be_bc[:, :], be[0:1, :].to_broadcast([P, D])).then_inc(be_loaded, 16)
            x_blocks = x_pad.rearrange("(b p) d -> p b d", p=P)
            for k, loaded in enumerate(x_loaded):
                sp.dma_start(x_in[:, 2 * k:2 * k + 2, :], x_blocks[:, 2 * k:2 * k + 2, :]).then_inc(loaded, 16)

            def write_table(l):
                for b in range(BLOCKS):
                    sp.wait_ge(staged, BLOCKS * l + b + 1)
                    for a, z, n in real_rows(b):
                        sp.dma_start(table[n:n + z - a, :], rows[a:z, STEP // 2 + b, :]).then_inc(table_written, 16)

            write_table(0)
            with sp.Fori(0, L) as l:
                wait_alone(sp, params_free, 3 * l + 3)
                sp.dma_start(eps_cur[:, :], eps[bass.ds(l, 1), :].to_broadcast([P, 1])).then_inc(params_loaded, 16)
                sp.dma_start(vec[:, :, :], vectors[bass.ds(l, 1), :, :, :].rearrange("o p v c -> p (o v) c")).then_inc(params_loaded, 16)
                sp.dma_start(W1_sb[:, :, :], W1[bass.ds(l, 1), :, :].rearrange("o (c p) d -> p (o c) d", p=P)).then_inc(params_loaded, 16)
                sp.dma_start(W2_sb[:, :, :], W2[bass.ds(l, 1), :, :].rearrange("o (c p) d -> p (o c) d", p=P)).then_inc(params_loaded, 16)
                sp.dma_start(b2_bc[:, :], b2[bass.ds(l, 1), :].to_broadcast([P, D])).then_inc(params_loaded, 16)
                sp.dma_start(be_bc[:, :], be[bass.ds(l + 1, 1), :].to_broadcast([P, D])).then_inc(params_loaded, 16)
                sp.dma_start(We_bc[:, :], We[bass.ds(l + 1, 1), :].to_broadcast([P, D])).then_inc(params_loaded, 16)
                with sp.If(l == L - 1):
                    for b in range(BLOCKS):
                        sp.wait_ge(ln_ready, b + 1)
                        for a, z, n in real_rows(b):
                            sp.dma_start(out[n:n + z - a, :], rows[a:z, b, :]).then_inc(out_written, 16)
                with sp.Else():
                    write_table(l + 1)
                sp.nop()
            sp.wait_ge(table_written, L * WRITES)
            sp.wait_ge(out_written, WRITES)

        @block.gpsimd
        def _(pool):
            nc.gpsimd.iota(cols[:, :], [[1, 2 * P]], base=0, channel_multiplier=0,
                           allow_small_or_imprecise_dtypes=True)
            nc.gpsimd.iota(part[:, :], [[0, 1]], base=0, channel_multiplier=1,
                           allow_small_or_imprecise_dtypes=True)
            nc.gpsimd.iota(node[:, :], [[P, BLOCKS]], base=-MARGIN, channel_multiplier=1,
                           allow_small_or_imprecise_dtypes=True)
            nc.gpsimd.iota(starts[:, :], [[WIN // 2, T_PAD // RUN], [0, RUN]], base=0, channel_multiplier=0,
                           allow_small_or_imprecise_dtypes=True).then_inc(iotas, 1)
            pool.wait_ge(iotas, 1)
            first = T - SHORT + SPLIT
            nc.gpsimd.iota(starts[:, first:T], [[0, T - first]], base=(T - SHORT) // RUN * (WIN // 2) + WIN // 2,
                           channel_multiplier=0, allow_small_or_imprecise_dtypes=True).then_inc(iotas, 1)
            nc.gpsimd.memset(hT[:, :, 0:GUARD], 0.0)
            nc.gpsimd.memset(carry[:, :], 0.0).then_inc(cleared, 1)

            def gather(quads, l, i):
                for q, quad in enumerate(quads):
                    if q % 4 == 0:
                        pool.wait_ge(cols_ready, 2 * BLOCKS * l + 2 * i + q // 4 + 1)
                    wait_alone(pool, quad_summed[q], quad_count(q, l, i) + 1)
                    for slot, tile, _ in quad:
                        nc.gpsimd.indirect_dma_start(
                            rows[:, slot, :], None, table[:, :],
                            bass.IndirectOffsetOnAxis(src_cur[:, tile:tile + 1], 0)).then_inc(landed[q], 16)

            pool.wait_ge(flag_ready, 1)
            slow = pool.value_load(flag[0:1, 0:1], min_val=0, max_val=1)
            with pool.Fori(0, L) as l:
                pool.wait_ge(table_written, WRITES * (l + 1))
                wait_alone(pool, x_updated, BLOCKS * l + 1)
                with pool.If(slow == 0):
                    with pool.Fori(0, BLOCKS - 1) as i:
                        gather(FULL, l, i)
                    gather(FINAL, l, BLOCKS - 1)
                with pool.Else():
                    with pool.Fori(0, T) as t:
                        wait_alone(pool, slow_cols, T * l + t + 1)
                        nc.gpsimd.indirect_dma_start(
                            rows[:, 0, :], None, table[:, :],
                            bass.IndirectOffsetOnAxis(src_one[:, 0:1], 0)).then_inc(slow_landed, 16)
                pool.nop()

        @block.scalar
        def _(act):
            act.dma_start(w_all[:, :], w_t).then_inc(w_loaded, 16)
            act.dma_start(src_all[:, :], src_t).then_inc(src_loaded, 16)
            act.dma_start(We_bc[:, :], We[0:1, :].to_broadcast([P, D])).then_inc(We_loaded, 16)

            def move_parts(step, h):
                nc.scalar.copy(w_parts_cur[:, h * PAIR:(h + 1) * PAIR, :],
                               w_parts[:, bass.ds(STEP * step + h * PAIR, PAIR), :]).then_inc(w_cols_ready[h], 1)

            act.wait_ge(w_parts_ready, 1)
            move_parts(0, 0)
            move_parts(0, 1)
            act.wait_ge(We_loaded, 16)
            nc.scalar.copy(We_ps[:, :], We_bc[:, :]).then_inc(We_ready, 1)

            def move_cols(step, h):
                nc.scalar.copy(src_cur[:, h * PAIR:(h + 1) * PAIR], src_all[:, bass.ds(STEP * step + h * PAIR, PAIR)])
                nc.scalar.copy(negw_cur[:, h * PAIR:(h + 1) * PAIR],
                               negw_all[:, bass.ds(STEP * step + h * PAIR, PAIR)]).then_inc(cols_ready, 1)

            act.wait_ge(src_loaded, 16)
            move_cols(0, 0)
            move_cols(0, 1)
            with act.Fori(0, BLOCKS) as i:
                for h in range(2):
                    act.wait_ge(w_summed[h], i + 2)
                    nc.scalar.mul(pair_w[:, h, bass.ds(i + 1, 1), :].rearrange("p o k -> p (o k)"),
                                  y_ps[h][:, 0:3], -1.0).then_inc(w_copied, 1)
                    move_parts(i + 1, h)
            for k, loaded in enumerate(x_loaded):
                act.wait_ge(loaded, 16)
                nc.scalar.copy(x_now[:, 2 * k:2 * k + 2, :], x_in[:, 2 * k:2 * k + 2, :]).then_inc(x_copied, 1)
            act.wait_ge(x_copied, len(x_loaded))
            act.wait_ge(w_placed, 1)
            nc.scalar.activation(w_sum[:, :], y_ps[2][:, 0:BLOCKS], ACT.Copy, scale=ok[:, 0:1]).then_inc(w_sum_ready, 1)
            act.wait_ge(w_sum_ready, 1)

            def scale_u(n, i):
                act.wait_ge(block_summed, n + 1)
                nc.scalar.copy(w_sum_cur[:, :], w_sum[:, bass.ds(i, 1)])
                nc.scalar.activation(u[:, :], x_now[:, bass.ds(i, 1), :].rearrange("p o d -> p (o d)"),
                                     ACT.Identity, scale=eps1[:, 0:1]).then_inc(u_scaled, 1)

            def copy_pair(h, n, summed, value):
                act.wait_ge(block_summed, n + 1)
                act.wait_ge(summed, value)
                nc.scalar.copy(pair_sb[:, h, :], pair_ps[h][:, :]).then_inc(pair_copied[h], 1)

            def finish_block(n, i):
                act.wait_ge(block_summed, n + 2)
                act.wait_ge(h_summed, n + 1)
                nc.scalar.copy(uT[:, :, :], uT_ps[:, :, :]).then_inc(uT_copied, 1)

            def finish_h(n, i):
                act.wait_ge(h_summed, n + 2)
                for c in range(C):
                    last = nc.scalar.activation(
                        hT[:, c:c + 1, bass.ds(P * i + GUARD - MARGIN, P)].rearrange("p o n -> p (o n)"),
                        h_ps[:, c, :], ACT.Identity, bias=vec[:, 0, c:c + 1])
                last.then_inc(h_copied, 1)

            act.wait_ge(flag_ready, 1)
            slow = act.value_load(flag[0:1, 0:1], min_val=0, max_val=1)
            with act.Fori(0, L) as l:
                act.wait_ge(params_loaded, PARAMS * (l + 1))
                nc.scalar.activation(eps1[:, :], eps_cur[:, :], ACT.Identity, bias=1.0).then_inc(eps_ready, 1)
                wait_alone(act, eps_ready, l + 1)
                with act.If(slow == 0):
                    with act.Fori(0, BLOCKS - 1) as i:
                        n = BLOCKS * l + i
                        scale_u(n, i)
                        act.wait_ge(v_ready[3], quad_count(3, l, i) + 1)
                        move_cols(i + 1, 0)
                        copy_pair(0, n, quad_summed[3], quad_count(3, l, i) + 2)
                        act.wait_ge(v_ready[7], quad_count(7, l, i) + 1)
                        move_cols(i + 1, 1)
                        copy_pair(1, n, quad_summed[7], quad_count(7, l, i) + 2)
                        finish_block(n, i)
                        nc.scalar.copy(carry[3 * P // 4:P, :], pair_sb[3 * P // 4:P, 1, :]).then_inc(carry_copied, 1)
                        finish_h(n, i)
                    i = BLOCKS - 1
                    n = BLOCKS * l + i
                    scale_u(n, i)
                    copy_pair(0, n, quad_summed[3], quad_count(3, l, i) + 2)
                    copy_pair(1, n, quad_summed[FQ - 1], quad_count(FQ - 1, l, i) + 2)
                    finish_block(n, i)
                    for c in range(C):
                        if c < C - 1:
                            act.wait_ge(h_part_summed, (C - 1) * l + c + 1)
                        else:
                            act.wait_ge(h_summed, n + 2)
                        nc.scalar.activation(hT[:, c, GUARD - MARGIN + P * i:GUARD - MARGIN + P * (i + 1)],
                                             last_h(c), ACT.Identity, bias=vec[:, 0, c:c + 1],
                                             ).then_inc(h_part_copied if c < C - 1 else h_copied, 1)
                with act.Else():
                    with act.Fori(0, T) as t:
                        act.wait_ge(slow_done, T * l + t + 1)
                        nc.scalar.copy(src_one[:, :], src_all[:, bass.ds(t, 1)])
                        nc.scalar.copy(row_one[:, :], row_all[:, bass.ds(t, 1)])
                        nc.scalar.copy(negw_one[:, :], negw_all[:, bass.ds(t, 1)]).then_inc(slow_cols, 1)
                    with act.Fori(0, BLOCKS) as i:
                        n = BLOCKS * l + i
                        scale_u(n, i)
                        finish_block(n, i)
                        finish_h(n, i)
                act.wait_ge(var_ready, l + 1)
                nc.scalar.activation(std[:, :], mv[:, :, 1], ACT.Sqrt, bias=eps_col[:, 0:1]).then_inc(std_ready, 1)
                act.wait_ge(bn_ready, l + 1)
                for b in range(BLOCKS):
                    at = GUARD - MARGIN + P * b
                    for c in range(C):
                        nc.scalar.activation(hT[:, c, at:at + P], hT[:, c, at:at + P], ACT.Relu,
                                             bias=bn_bias[:, c:c + 1], scale=bn_scale[:, c:c + 1]).then_inc(hr_ready, 1)
                nc.scalar.copy(We_ps[:, :], We_bc[:, :]).then_inc(We_ready, 1)
                move_cols(0, 0)
                move_cols(0, 1)
                with act.If(l == L - 1):
                    for b in range(BLOCKS):
                        act.wait_ge(ln_var_ready, b + 1)
                        nc.scalar.activation(ln_std[:, b:b + 1], ln_mv[:, b, 1:2], ACT.Sqrt,
                                             bias=eps_col[:, 0:1]).then_inc(ln_std_ready, 1)
                with act.Else():
                    for b in range(BLOCKS):
                        act.wait_ge(y_added, BLOCKS * l + b + 1)
                        nc.scalar.activation(x_now[:, b, :], y_stage(b), ACT.Relu,
                                             scale=mask[:, b:b + 1]).then_inc(x_updated, 1)
                    wait_alone(act, x_updated, BLOCKS * (l + 1) + 1)
                act.sem_inc(params_free, 1)

        @block.vector
        def _(dve):
            done = [0]

            def then_wait(ins):
                done[0] += 1
                ins.then_inc(prep, 1)
                dve.wait_ge(prep, done[0])

            nc.vector.memset(ones[:, :], 1.0)
            nc.vector.memset(eps_col[:, :], EPS)
            nc.vector.memset(pair_w[:, :, 0:1, :], 0.0)
            nc.vector.memset(w_parts[:, T_PAD:, :], 0.0)
            for s in w_summed + quad_summed + pair_copied + [carry_copied, block_summed, uT_copied, h_summed,
                                                             h_copied, slow_done, x_updated]:
                dve.sem_inc(s, 1)
            dve.wait_ge(dst_loaded, 16)
            then_wait(nc.vector.tensor_scalar(row_all[:, :], dst_all[:, :], float(MARGIN), None, ALU.add))
            dve.wait_ge(iotas, 2)
            then_wait(nc.vector.tensor_tensor(local_all[:, :], row_all[:, :], starts[:, :], ALU.subtract))
            then_wait(nc.vector.tensor_scalar(outside[:, :], local_all[:, :], 0.0, None, ALU.is_lt))
            nc.vector.scalar_tensor_tensor(outside[:, :], local_all[:, :], float(WIN - 1), outside[:, :],
                                           ALU.is_gt, ALU.add, accum_out=bad[:, :]).then_inc(bad_counted, 1)
            dve.wait_ge(w_loaded, 16)
            then_wait(nc.vector.tensor_scalar(negw_all[:, :], w_all[:, :], -1.0, None, ALU.mult))
            left = negw_all
            for k in range(3):
                then_wait(nc.vector.tensor_copy(w_parts[:, 0:T_PAD, k], left[:, :]))
                if k < 2:
                    then_wait(nc.vector.tensor_tensor(rest[:, :], left[:, :], w_parts[:, 0:T_PAD, k], ALU.subtract))
                    left = rest
            dve.sem_inc(w_parts_ready, 1)
            dve.wait_ge(bad_summed, 1)
            then_wait(nc.vector.tensor_scalar(ok[:, :], y_ps[2][:, BLOCKS:BLOCKS + 1], 0.0, None, ALU.is_equal))
            nc.vector.tensor_scalar(flag[:, :], ok[0:1, 0:1], 0.0, None, ALU.is_equal).then_inc(flag_ready, 1)

            def make_onehot(i, h, to, ready):
                nc.vector.tensor_tensor(
                    to[:, h, :, :], cols[:, 0:WIN].unsqueeze(1).to_broadcast([P, PAIR, WIN]),
                    local_all[:, bass.ds(STEP * i + h * PAIR, PAIR)].unsqueeze(2).to_broadcast([P, PAIR, WIN]),
                    ALU.is_equal).then_inc(ready, 1)

            dve.wait_ge(be_loaded, 16)
            for k, loaded in enumerate(x_loaded):
                dve.wait_ge(loaded, 16)
                for b in (2 * k, 2 * k + 1):
                    nc.vector.tensor_tensor(table_stage(b), x_in[:, b, :], be_bc[:, :], ALU.add).then_inc(staged, 1)
            nc.vector.tensor_scalar(ident[:, :], cols[:, 0:P], part[:, 0:1], None, ALU.is_equal)
            nc.vector.tensor_scalar(mask_lo[:, :], node[:, :], 0.0, None, ALU.is_ge)
            then_wait(nc.vector.tensor_scalar(upper[:, :], part[:, :], float(WIN), -float(WIN - 2 * MARGIN),
                                              ALU.is_ge, ALU.mult))
            nc.vector.scalar_tensor_tensor(mask[:, :], node[:, :], float(N), mask_lo[:, :], ALU.is_lt, ALU.mult)
            then_wait(nc.vector.scalar_tensor_tensor(target[:, :], part[:, :], float(WIN), upper[:, :],
                                                     ALU.add, ALU.add))
            nc.vector.tensor_scalar(place[:, :], cols[:, :], target[:, 0:1], None,
                                    ALU.is_equal).then_inc(masks_ready, 1)
            dve.wait_ge(staged, BLOCKS)
            dve.wait_ge(We_ready, 1)
            dve.sem_inc(params_free, 3)
            with dve.Fori(0, BLOCKS) as i:
                for h in range(2):
                    dve.wait_ge(w_summed[h], i + 1)
                    make_onehot(i, h, onehot_bf, w_onehot_ready[h])
            def messages(quads, q, l, i):
                quad = quads[q]
                dve.wait_ge(landed[q], landed_count(q, l, i) + 16 * len(quad))
                for slot, tile, _ in quad:
                    last = nc.vector.scalar_tensor_tensor(rows[:, slot, :], We_ps[:, :], negw_cur[:, tile:tile + 1],
                                                          rows[:, slot, :], ALU.mult, ALU.max)
                last.then_inc(v_ready[q], 1)

            def finish_u(n, ready):
                dve.wait_ge(u_scaled, n + 1)
                return nc.vector.scalar_tensor_tensor(u[:, :], We_ps[:, :], w_sum_cur[:, 0:1], u[:, :],
                                                      ALU.mult, ALU.add).then_inc(ready, 1)

            def block_stats(n, i):
                dve.wait_ge(h_copied, n + 1)
                for c in range(C):
                    last = nc.vector.bn_stats(stats[:, c, bass.ds(i, 1), :].rearrange("p o s -> p (o s)"),
                                              hT[:, c:c + 1, bass.ds(P * i, P)].rearrange("p o n -> p (o n)"))
                return last

            def late_stats(slot, a, z):
                for c in range(C):
                    last = nc.vector.bn_stats(stats[:, c, slot, :], hT[:, c, a:z])
                return last

            def edge_step(quads, l, i):
                n = BLOCKS * l + i
                for h in range(2):
                    for q in ([3] if h == 0 else [FQ - 1, 7]):
                        dve.wait_ge(quad_summed[q], quad_count(q, l, i) + 1)
                    make_onehot(i, h, onehot, onehot_ready)
                    dve.wait_ge(cols_ready, 2 * BLOCKS * l + 2 * i + h + 1)
                    for q in range(4 * h, min(4 * h + 4, len(quads))):
                        messages(quads, q, l, i)
                        if q == 2:
                            finish_u(n, u_ready)
                        if q == 5:
                            block_stats(n, i)
                            if quads is FINAL:
                                late_stats(BLOCKS, GUARD + (BLOCKS - 2) * P, GUARD - MARGIN + (BLOCKS - 1) * P)

            dve.wait_ge(flag_ready, 1)
            slow = dve.value_load(flag[0:1, 0:1], min_val=0, max_val=1)
            with dve.Fori(0, L) as l:
                dve.wait_ge(x_updated, BLOCKS * l + 1)
                dve.wait_ge(cleared, 1)
                nc.vector.memset(carry[3 * P // 4:P, :], 0.0).then_inc(carry_cleared, 1)
                wait_alone(dve, We_ready, l + 1)
                with dve.If(slow == 0):
                    with dve.Fori(0, BLOCKS - 1) as i:
                        edge_step(FULL, l, i)
                    edge_step(FINAL, l, BLOCKS - 1)
                    for c in range(C):
                        if c < C - 1:
                            dve.wait_ge(h_part_copied, (C - 1) * l + c + 1)
                        else:
                            dve.wait_ge(h_copied, BLOCKS * l + BLOCKS + 1)
                        last = nc.vector.bn_stats(stats[:, c, BLOCKS + 1, :],
                                                  hT[:, c, GUARD - MARGIN + (BLOCKS - 1) * P:GUARD + N])
                    last.then_inc(stats_done, 1)
                with dve.Else():
                    sums = rows[:, SLOW_SUMS:SLOW_SUMS + BLOCKS, :]
                    dve.wait_ge(table_written, WRITES * (l + 1))
                    nc.vector.memset(sums, 0.0).then_inc(slow_cleared, 1)
                    wait_alone(dve, slow_cleared, l + 1)
                    with dve.Fori(0, T) as t:
                        k0 = (2 + BLOCKS) * (T * l + t)
                        dve.wait_ge(slow_landed, 16 * (T * l + t + 1))
                        nc.vector.scalar_tensor_tensor(rows[:, 0, :], We_ps[:, :], negw_one[:, 0:1], rows[:, 0, :],
                                                       ALU.mult, ALU.max).then_inc(slow_chain, 1)
                        dve.wait_ge(slow_chain, k0 + 1)
                        nc.vector.scalar_tensor_tensor(rows[:, 1, :], We_ps[:, :], negw_one[:, 0:1], rows[:, 0, :],
                                                       ALU.mult, ALU.subtract).then_inc(slow_chain, 1)
                        for b in range(BLOCKS):
                            m = BLOCKS * (T * l + t) + b
                            dve.wait_ge(slow_chain, k0 + 2 + b)
                            nc.vector.tensor_scalar(onehot_block[:, :], cols[:, 0:P], float(P * b), row_one[:, 0:1],
                                                    ALU.add, ALU.is_equal).then_inc(slow_onehot, 1)
                            dve.wait_ge(slow_summed, m + 1)
                            nc.vector.tensor_tensor(sums[:, b, :], sums[:, b, :], y_ps[0][:, :],
                                                    ALU.subtract).then_inc(slow_chain, 1)
                        dve.wait_ge(slow_chain, k0 + 2 + BLOCKS)
                        dve.sem_inc(slow_done, 1)
                    with dve.Fori(0, BLOCKS) as i:
                        n = BLOCKS * l + i
                        finish_u(n, slow_u)
                        dve.wait_ge(slow_u, n + 1)
                        nc.vector.tensor_tensor(
                            u[:, :], rows[:, bass.ds(SLOW_SUMS + i, 1), :].rearrange("p o d -> p (o d)"), u[:, :],
                            ALU.add).then_inc(u_ready, 1)
                        block_stats(n, i)
                    dve.wait_ge(h_copied, BLOCKS * l + BLOCKS + 1)
                    late_stats(BLOCKS, GUARD + (BLOCKS - 2) * P, GUARD - MARGIN + (BLOCKS - 1) * P)
                    late_stats(BLOCKS + 1, GUARD - MARGIN + (BLOCKS - 1) * P, GUARD + N).then_inc(stats_done, 1)
                wait_alone(dve, stats_done, l + 1)
                for c in range(C):
                    last = nc.vector.bn_aggr(mv[:, c, :], stats[:, c, 2:BLOCKS + 2, :].rearrange("p s k -> p (s k)"))
                last.then_inc(var_ready, 1)
                dve.wait_ge(std_ready, l + 1)
                nc.vector.reciprocal(rstd[:, :], std[:, :]).then_inc(bn_chain, 1)
                dve.wait_ge(bn_chain, 3 * l + 1)
                dve.wait_ge(params_loaded, PARAMS * (l + 1))
                nc.vector.tensor_tensor(bn_scale[:, :], rstd[:, :], vec[:, 1, :], ALU.mult).then_inc(bn_chain, 1)
                dve.wait_ge(bn_chain, 3 * l + 2)
                nc.vector.tensor_tensor(bn_shift[:, :], mv[:, :, 0], bn_scale[:, :], ALU.mult).then_inc(bn_chain, 1)
                dve.wait_ge(bn_chain, 3 * l + 3)
                nc.vector.tensor_tensor(bn_bias[:, :], vec[:, 2, :], bn_shift[:, :], ALU.subtract).then_inc(bn_ready, 1)

                def add_b2(b):
                    dve.wait_ge(y_summed, BLOCKS * l + b + 1)
                    nc.vector.tensor_tensor(y_stage(b), y_ps[b % 3][:, :], b2_bc[:, :], ALU.add).then_inc(y_added, 1)
                    dve.wait_ge(y_added, BLOCKS * l + b + 1)

                with dve.If(l == L - 1):
                    def ln_second(b):
                        dve.wait_ge(ln_std_ready, b + 1)
                        nc.vector.reciprocal(ln_rstd[:, b:b + 1], ln_std[:, b:b + 1]).then_inc(ln_scaled, 1)
                        dve.wait_ge(ln_scaled, b + 1)
                        nc.vector.tensor_scalar(y_stage(b), table_stage(b), ln_mv[:, b, 0:1], ln_rstd[:, b:b + 1],
                                                ALU.subtract, ALU.mult).then_inc(ln_ready, 1)

                    for b in range(BLOCKS):
                        add_b2(b)
                        nc.vector.scalar_tensor_tensor(table_stage(b), y_stage(b), 0.0, x_in[:, b, :],
                                                       ALU.max, ALU.add).then_inc(ln_chain, 1)
                        dve.wait_ge(ln_chain, 2 * b + 1)
                        nc.vector.bn_stats(ln_stats[:, b, :], table_stage(b)).then_inc(ln_chain, 1)
                        dve.wait_ge(ln_chain, 2 * b + 2)
                        nc.vector.bn_aggr(ln_mv[:, b, :], ln_stats[:, b, :]).then_inc(ln_var_ready, 1)
                        if b:
                            ln_second(b - 1)
                    ln_second(BLOCKS - 1)
                with dve.Else():
                    for b in range(BLOCKS):
                        add_b2(b)
                        nc.vector.scalar_tensor_tensor(table_stage(b), y_stage(b), 0.0, be_bc[:, :],
                                                       ALU.max, ALU.add).then_inc(staged, 1)
                    wait_alone(dve, staged, BLOCKS * (l + 2))
                dve.sem_inc(params_free, 1)

        @block.tensor
        def _(pe):
            pe.wait_ge(bad_counted, 1)
            nc.tensor.matmul(y_ps[2][:, BLOCKS:BLOCKS + 1], ones[:, :], bad[:, :],
                             start=True, stop=True).then_inc(bad_summed, 1)
            def sum_w(quads, h, i):
                pe.wait_ge(w_onehot_ready[h], i + 1)
                pe.wait_ge(w_cols_ready[h], i + 1)
                tiles, firsts, lasts = tiles_of(quads, h)
                for t in tiles:
                    _, tile, win = t
                    last = nc.tensor.matmul(y_ps[h][WIN * win:WIN * (win + 1), 0:3],
                                            onehot_bf[:, h, tile - h * PAIR, :], w_parts_cur[:, tile, :],
                                            start=t in firsts, stop=t in lasts)
                last.then_inc(w_summed[h], 1)

            with pe.Fori(0, BLOCKS - 1) as i:
                sum_w(FULL, 0, i)
                sum_w(FULL, 1, i)
            sum_w(FINAL, 0, BLOCKS - 1)
            sum_w(FINAL, 1, BLOCKS - 1)
            pe.wait_ge(masks_ready, 1)
            pe.wait_ge(flag_ready, 1)
            pe.wait_ge(w_copied, 2 * BLOCKS)
            sources = [(WIN, 0, 1), (0, 1, 1), (P, 1, 0)]
            for k in range(3):
                for m, (at, h, first) in enumerate(sources):
                    last = nc.tensor.matmul(y_ps[2][:, 0:BLOCKS], place[:, at:at + P],
                                            pair_w[:, h, first:first + BLOCKS, k],
                                            start=(k == 0 and m == 0), stop=(k == 2 and m == 2))
            last.then_inc(w_placed, 1)

            def sum_pair(quads, h, l, i):
                pe.wait_ge(pair_copied[h], BLOCKS * l + i + 1)
                pe.wait_ge(onehot_ready, 2 * BLOCKS * l + 2 * i + h + 1)
                _, firsts, lasts = tiles_of(quads, h)
                for q in range(4 * h, min(4 * h + 4, len(quads))):
                    pe.wait_ge(v_ready[q], quad_count(q, l, i) + 1)
                    for t in quads[q]:
                        slot, tile, win = t
                        last = nc.tensor.matmul(pair_ps[h][WIN * win:WIN * (win + 1), :],
                                                onehot[:, h, tile - h * PAIR, :], rows[:, slot, :],
                                                start=t in firsts, stop=t in lasts)
                    last.then_inc(quad_summed[q], 1)
                    if q == 4:
                        open_block(BLOCKS * l + i, l, i, True)

            def open_block(n, l, i, pairs):
                pe.wait_ge(u_ready, n + 1)
                pe.wait_ge(uT_copied, n + 1)
                chunks = [slice(c * P, (c + 1) * P) for c in range(C)]
                for c, f in enumerate(chunks):
                    last = nc.tensor.matmul(uT_ps[:, c, :], u[:, f], ident[:, :], start=(c == 0),
                                            stop=not pairs, skip_group_check=True)
                if not pairs:
                    last.then_inc(block_summed, 1)
                    return
                pe.wait_ge(carry_cleared, l + 1)
                pe.wait_ge(carry_copied, (BLOCKS - 1) * l + i + 1)
                for c, f in enumerate(chunks):
                    nc.tensor.matmul(uT_ps[:, c, 0:PLACED - WIN], carry[:, f], place[:, P:WIN + PLACED],
                                     start=False, stop=False, skip_group_check=True)
                pe.wait_ge(pair_copied[0], n + 2)
                for c, f in enumerate(chunks):
                    nc.tensor.matmul(uT_ps[:, c, 0:PLACED], pair_sb[:, 0, f], place[:, WIN:WIN + PLACED],
                                     start=False, stop=False, skip_group_check=True)

            def close_block(n):
                pe.wait_ge(pair_copied[1], n + 2)
                for c in range(C):
                    last = nc.tensor.matmul(uT_ps[:, c, WIN:P], pair_sb[:, 1, c * P:(c + 1) * P],
                                            place[:, WIN:P], start=False, stop=True, skip_group_check=True)
                last.then_inc(block_summed, 1)

            def product_h(n, l, apart=False):
                pe.wait_ge(params_loaded, PARAMS * (l + 1))
                pe.wait_ge(uT_copied, n + 2)
                pe.wait_ge(h_copied, n + 1)
                for c in range(C):
                    for k in range(C):
                        last = nc.tensor.matmul(last_h(c) if apart else h_ps[:, c, :],
                                                W1_sb[:, k, c * P:(c + 1) * P], uT[:, k, :],
                                                start=(k == 0), stop=(k == C - 1))
                    if c == C - 1:
                        last.then_inc(h_summed, 1)
                    elif apart:
                        last.then_inc(h_part_summed, 1)

            pe.wait_ge(flag_ready, 1)
            slow = pe.value_load(flag[0:1, 0:1], min_val=0, max_val=1)
            with pe.Fori(0, L) as l:
                with pe.If(slow == 0):
                    with pe.Fori(0, BLOCKS - 1) as i:
                        sum_pair(FULL, 0, l, i)
                        sum_pair(FULL, 1, l, i)
                        close_block(BLOCKS * l + i)
                        product_h(BLOCKS * l + i, l)
                    i = BLOCKS - 1
                    sum_pair(FINAL, 0, l, i)
                    sum_pair(FINAL, 1, l, i)
                    close_block(BLOCKS * l + i)
                    product_h(BLOCKS * l + i, l, apart=True)
                with pe.Else():
                    with pe.Fori(0, T) as t:
                        for b in range(BLOCKS):
                            pe.wait_ge(slow_onehot, BLOCKS * (T * l + t) + b + 1)
                            nc.tensor.matmul(y_ps[0][:, :], onehot_block[:, :], rows[:, 1, :],
                                             start=True, stop=True).then_inc(slow_summed, 1)
                    with pe.Fori(0, BLOCKS) as i:
                        open_block(BLOCKS * l + i, l, i, False)
                        product_h(BLOCKS * l + i, l)
                for b in range(BLOCKS):
                    if b > 0:
                        pe.wait_ge(hr_ready, C * (BLOCKS * l + b + 1))
                    if b >= 3:
                        pe.wait_ge(y_added, BLOCKS * l + b - 2)
                    at = GUARD - MARGIN + P * b
                    for c in range(C):
                        if b == 0:
                            pe.wait_ge(hr_ready, C * BLOCKS * l + c + 1)
                        last = nc.tensor.matmul(y_ps[b % 3][:, :], hT[:, c, at:at + P], W2_sb[:, c, :],
                                                start=(c == 0), stop=(c == C - 1))
                    last.then_inc(y_summed, 1)
                pe.wait_ge(y_summed, BLOCKS * (l + 1))
                pe.sem_inc(params_free, 1)


def kernel(**inputs):
    import numpy as np
    import concourse.bacc as bacc
    from concourse.bass_utils import run_bass_kernel_spmd

    P, STEP, MARGIN = 128, 32, 16
    x = np.asarray(inputs["x"])
    N, D = x.shape
    src, dst, w = (np.asarray(inputs[k]).reshape(-1) for k in ("src", "dst", "edge_weight1"))
    blocks = -(-(N + MARGIN) // P)
    edges = blocks * STEP * P

    def padded(a, size, fill, before=0):
        out = np.full((size,) + a.shape[1:], fill, a.dtype)
        out[before:before + a.shape[0]] = a
        return out

    def by_tile(a, fill):
        return np.ascontiguousarray(padded(a, edges, fill).reshape(-1, P).T)

    We, be, W1, b1, gamma, beta, W2, b2, eps = (
        np.asarray(inputs["L0_gnn_" + k]) for k in ("We", "be", "W1", "b1", "gamma", "beta", "W2", "b2", "eps"))
    L = W1.shape[0]
    vectors = np.stack([v.reshape(L, D // P, P).transpose(0, 2, 1) for v in (b1, gamma, beta)], axis=2)
    arrays = {
        "x_pad": padded(x, blocks * P, 0, before=MARGIN),
        "src_t": by_tile(src, 0),
        "dst_t": by_tile(dst, N),
        "w_t": by_tile(w, 0),
        "We": padded(We.reshape(L, D), L + 1, 0),
        "be": padded(be, L + 1, 0),
        "W1": W1, "W2": W2, "b2": b2,
        "vectors": np.ascontiguousarray(vectors),
        "eps": eps.reshape(L, 1),
    }
    nc = bacc.Bacc("TRN2", target_bir_lowering=False, num_devices=1)
    args = [nc.dram_tensor(name, a.shape, mybir.dt.from_np(a.dtype), kind="ExternalInput").ap()
            for name, a in arrays.items()]
    out = nc.dram_tensor("out", (N, D), mybir.dt.float32, kind="ExternalOutput").ap()
    gnn_layers(nc, *args, out)
    result = run_bass_kernel_spmd(nc, [arrays], core_ids=[0])
    return result.results[0]["out"]
```

```python
import numpy as np

import concourse.bass as bass
from concourse import mybir
from contextlib import ExitStack



def gnn_layers(nc, x_pad, src_t, src_late, dst_t, w_t, We, be, W1, W2, b2, vectors, eps, out):
    fp32 = mybir.dt.float32
    bf16 = mybir.dt.bfloat16
    i32 = mybir.dt.int32
    ALU = mybir.AluOpType
    ACT = mybir.ActivationFunctionType

    P = 128
    L, D, _ = W1.shape
    C = D // P
    N = out.shape[0]
    BLOCKS = x_pad.shape[0] // P
    T_PAD = src_t.shape[1]
    EDGES = 32 * N
    WIN, RUN, MARGIN = 64, 8, 16
    PAIR = 2 * RUN
    STEP = 2 * PAIR
    T = -(-EDGES // P)
    LAST = T - (BLOCKS - 1) * STEP
    assert T_PAD == BLOCKS * STEP and STEP * P == P * EDGES // N
    QUADS = STEP // 4
    EPS = 1e-05
    TAIL = N - (BLOCKS - 1) * P + MARGIN
    WARM = 4
    GAP = 4
    GUARD = 2 * P
    PLACED = WIN + 2 * MARGIN

    table = nc.dram_tensor("node_table", (N, D), fp32, kind="Internal").ap()

    def quads_of(tiles, pair, sizes, split=RUN):
        ends = np.cumsum(sizes)
        return [[(pair * PAIR + 4 * q + k, pair * PAIR + j, int(j >= split))
                 for k, j in enumerate(tiles[end - size:end])]
                for q, (size, end) in enumerate(zip(sizes, ends))]

    alternating = [k // 2 + RUN * (k % 2) for k in range(PAIR)]
    FULL = quads_of(alternating, 0, [4] * 4) + quads_of(alternating, 1, [4] * 4)
    GATHERED = STEP - 1
    FULL_GATHERS = [sum(tile != GATHERED for _, tile, _ in quad) for quad in FULL]
    SHARE = [0, 8, 0, 8, 4, 10, 0, 0]
    assert sum(SHARE) == 3 * BLOCKS
    SHORT = LAST - PAIR
    SPLIT = (SHORT + 1) // 2
    short = [k // 2 + SPLIT * (k % 2) for k in range(SHORT)]
    FINAL = quads_of(alternating, 0, [4] * 4) + quads_of(short, 1, [SHORT - 6, 3, 2, 1], SPLIT)

    def tiles_of(quads, h):
        tiles = [t for q in quads[4 * h:4 * h + 4] for t in q]
        windows = [[t for t in tiles if t[2] == win] for win in (0, 1)]
        return tiles, [w[0] for w in windows], [w[-1] for w in windows]

    ctx = ExitStack()
    with ctx:
        def sb(name, shape, dt=fp32):
            return ctx.enter_context(nc.sbuf_tensor(name, shape, dt))

        def sem(name):
            return ctx.enter_context(nc.semaphore(name))

        rows = sb("rows", [P, STEP, D])
        onehot = sb("onehot", [P, 2, PAIR, WIN])
        x_now = sb("x_now", [P, BLOCKS, D])
        table_parts = sb("table_parts", [P, 3, BLOCKS, D], bf16)
        src_bc = sb("src_bc", [P, BLOCKS - 1, P], i32)
        src_onehot = sb("src_onehot", [P, BLOCKS, P], bf16)
        hT = sb("hT", [P, C, GUARD - MARGIN + BLOCKS * P])
        W1_sb = sb("W1_sb", [P, C, D])
        W2_sb = sb("W2_sb", [P, C, D])
        b2_bc = sb("b2_bc", [P, D])
        be_bc = sb("be_bc", [P, D])
        We_bc = sb("We_bc", [P, D])
        pair_sb = sb("pair_sb", [P, 2, D])
        carry = sb("carry", [P, D])
        u = sb("u", [P, D])
        uT = sb("uT", [P, C, P])
        src_all = sb("src_all", [P, T_PAD], i32)
        dst_all = sb("dst_all", [P, T_PAD], i32)
        w_all = sb("w_all", [P, T_PAD])
        rest = sb("rest", [P, T_PAD])
        w_parts = sb("w_parts", [P, T_PAD + STEP, 3], bf16)
        w_parts_cur = sb("w_parts_cur", [P, STEP, 3], bf16)
        onehot_bf = sb("onehot_bf", [P, 2, PAIR, WIN], bf16)
        negw_all = sb("negw_all", [P, T_PAD])
        row_all = sb("row_all", [P, T_PAD])
        local_all = sb("local_all", [P, T_PAD])
        starts = sb("starts", [P, T_PAD])
        src_cur = sb("src_cur", [P, STEP], i32)
        negw_cur = sb("negw_cur", [P, STEP])
        cols = sb("cols", [P, 2 * P])
        part = sb("part", [P, 1])
        upper = sb("upper", [P, 1])
        target = sb("target", [P, 1])
        ident = sb("ident", [P, P])
        place = sb("place", [P, 2 * P])
        ones = sb("ones", [P, P])
        node = sb("node", [P, BLOCKS])
        mask = sb("mask", [P, BLOCKS])
        mask_lo = sb("mask_lo", [P, BLOCKS])
        bad = sb("bad", [P, 1])
        ok = sb("ok", [P, 1])
        flag = sb("flag", [1, 1], i32)
        pair_w = sb("pair_w", [P, 3, 3])
        last_pair_w = sb("last_pair_w", [P, 2, 3])
        w_sum = sb("w_sum", [P, BLOCKS])
        w_sum_cur = sb("w_sum_cur", [P, 1])
        vec = sb("vec", [P, 3, C])
        eps_cur = sb("eps_cur", [P, 1])
        eps1 = sb("eps1", [P, 1])
        stats = sb("stats", [P, C, BLOCKS + 2, 6])
        mv = sb("mv", [P, C, 2])
        eps_col = sb("eps_col", [P, 1])
        std = sb("std", [P, C])
        unread = sb("unread", [P, 1])
        rstd = sb("rstd", [P, C])
        bn_scale = sb("bn_scale", [P, C])
        bn_shift = sb("bn_shift", [P, C])
        bn_bias = sb("bn_bias", [P, C])
        ln_stats = sb("ln_stats", [P, BLOCKS, 6])
        ln_mv = sb("ln_mv", [P, BLOCKS, 2])
        ln_std = sb("ln_std", [P, BLOCKS])
        ln_rstd = sb("ln_rstd", [P, BLOCKS])
        src_one = sb("src_one", [P, 1], i32)
        negw_one = sb("negw_one", [P, 1])
        row_one = sb("row_one", [P, 1])
        onehot_block = sb("onehot_block", [P, P])

        def pb(name, shape):
            return ctx.enter_context(nc.psum_tensor(name, shape, fp32))

        We_ps = pb("We_ps", [P, D])
        pair_ps = [pb(f"pair_ps{h}", [P, D]) for h in range(2)]
        uT_ps = pb("uT_ps", [P, C, P])
        h_ps = pb("h_ps", [P, C, P])
        y_ps = [pb(f"y_ps{b}", [P, D]) for b in range(3)]

        x_loaded = [sem(f"x_loaded{k}") for k in range(BLOCKS // 2)]
        dst_loaded = sem("dst_loaded")
        w_loaded = sem("w_loaded")
        src_loaded = sem("src_loaded")
        be_loaded = sem("be_loaded")
        We_loaded = sem("We_loaded")
        iotas = sem("iotas")
        cleared = sem("cleared")
        prep = sem("prep")
        masks_ready = sem("masks_ready")
        w_cols_ready = [sem(f"w_cols_ready{h}") for h in range(2)]
        w_onehot_ready = [sem(f"w_onehot_ready{h}") for h in range(2)]
        w_summed = [sem(f"w_summed{h}") for h in range(2)]
        negw_ready = sem("negw_ready")
        w_parts_ready = sem("w_parts_ready")
        w_copied = sem("w_copied")
        bad_counted = sem("bad_counted")
        bad_summed = sem("bad_summed")
        w_shifted = sem("w_shifted")
        w_placed = sem("w_placed")
        w_sum_ready = sem("w_sum_ready")
        src_bc_loaded = sem("src_bc_loaded")
        x_reloaded = [sem(f"x_reloaded{k}") for k in range(BLOCKS // 2)]
        src_onehot_ready = sem("src_onehot_ready")
        tile_gathered = sem("tile_gathered")
        tile_moved = sem("tile_moved")
        early_split = [sem(f"early_split{k}") for k in range(2)]
        split = [sem(f"split{k}") for k in range(4)]
        flag_ready = sem("flag_ready")
        We_ready = sem("We_ready")
        staged = sem("staged")
        table_written = sem("table_written")
        params_free = sem("params_free")
        params_loaded = sem("params_loaded")
        cols_ready = sem("cols_ready")
        landed = [sem(f"landed{q}") for q in range(QUADS)]
        v_ready = [sem(f"v_ready{q}") for q in range(QUADS)]
        quad_summed = [sem(f"quad_summed{q}") for q in range(QUADS)]
        onehot_ready = sem("onehot_ready")
        pair_copied = [sem(f"pair_copied{h}") for h in range(2)]
        carry_cleared = sem("carry_cleared")
        carry_copied = sem("carry_copied")
        eps_ready = sem("eps_ready")
        u_scaled = sem("u_scaled")
        u_ready = sem("u_ready")
        block_summed = sem("block_summed")
        uT_copied = sem("uT_copied")
        h_summed = sem("h_summed")
        h_copied = sem("h_copied")
        h_part_summed = sem("h_part_summed")
        h_part_copied = sem("h_part_copied")
        stats_done = sem("stats_done")
        var_ready = sem("var_ready")
        std_ready = sem("std_ready")
        ln_var_ready = sem("ln_var_ready")
        ln_std_ready = sem("ln_std_ready")
        bn_chain = sem("bn_chain")
        bn_ready = sem("bn_ready")
        hr_ready = sem("hr_ready")
        y_summed = sem("y_summed")
        y_added = sem("y_added")
        x_updated = sem("x_updated")
        half_summed = sem("half_summed")
        half_added = sem("half_added")
        half_staged = sem("half_staged")
        ln_chain = sem("ln_chain")
        ln_scaled = sem("ln_scaled")
        ln_ready = sem("ln_ready")
        out_written = sem("out_written")
        slow_cols = sem("slow_cols")
        slow_landed = sem("slow_landed")
        slow_chain = sem("slow_chain")
        slow_onehot = sem("slow_onehot")
        slow_summed = sem("slow_summed")
        slow_done = sem("slow_done")
        slow_cleared = sem("slow_cleared")
        slow_u = sem("slow_u")
        waited = sem("waited")

        def y_stage(b):
            return rows[:, b, :]

        def table_stage(b):
            return rows[:, STEP // 2 + b, :]

        def rest_stage(k):
            return rows[:, BLOCKS + k % (STEP // 2 - BLOCKS), :]

        def x_slot(b):
            return BLOCKS + b if b < STEP // 2 - BLOCKS else STEP // 2 + 4 + b

        def last_h(c):
            return h_ps[:, 0, :] if c == 0 else y_ps[c - 1][:, 0:P]

        SLOW_SUMS = 8

        def real_rows(b):
            lo = MARGIN if b == 0 else 0
            hi = TAIL if b == BLOCKS - 1 else P
            cuts = [lo, hi] if hi % 16 == 0 else [lo, hi - hi % 16, hi]
            return [(a, z, b * P - MARGIN + a) for a, z in zip(cuts, cuts[1:])]

        WRITES = 16 * sum(len(real_rows(b)) for b in range(BLOCKS))
        PARAMS = 16 * 7

        def landed_count(q, l, i):
            return 16 * (FULL_GATHERS[q] * (BLOCKS - 1) + len(FINAL[q])) * l + 16 * FULL_GATHERS[q] * i

        ORDER = [BLOCKS - 1] + list(range(BLOCKS - 1))

        MORE_WRITES = WRITES + 16 * len(real_rows(ORDER[-1]))
        HALVES = [slice(0, D // 2), slice(D // 2, D)]

        def y_half(h):
            return y_ps[(BLOCKS - 1 + h) % 3][:, HALVES[h]]

        FEW = 2
        GROUPS = [slice(0, FEW), slice(FEW, C)]
        LAG = 4
        AHEAD = 3
        HR_ORDER = [(m, c) for g in GROUPS for m in range(AHEAD) for c in range(C)[g]]
        HR_ORDER += [(m, c) for m in range(AHEAD, BLOCKS) for c in range(C)]

        EARLY = 4

        def first_part(k, n):
            nc.scalar.copy(table_parts[:, 0, ORDER[k], :], table_stage(ORDER[k])).then_inc(split[0], 1)

        def take_rest(engine, ops, k, n, ready):
            b = ORDER[k]
            engine.wait_ge(split[0], n + k + 1)
            ops.tensor_tensor(rest_stage(k), table_stage(b), table_parts[:, 0, b, :], ALU.subtract).then_inc(ready, 1)

        def second_part(act, k, n, rest_taken):
            act.wait_ge(rest_taken, n + k + 1)
            nc.scalar.copy(table_parts[:, 1, ORDER[k], :], rest_stage(k)).then_inc(split[2], 1)

        def third_part(engine, ops, k, n, ready):
            b = ORDER[k]
            engine.wait_ge(split[2], n + k + 1)
            ops.tensor_tensor(table_parts[:, 2, b, :], rest_stage(k), table_parts[:, 1, b, :],
                              ALU.subtract).then_inc(ready, 1)

        def split_table(engine, ops, places, rest_taken, ready):
            take_rest(engine, ops, places[0], 0, rest_taken)
            for k in places[1:]:
                take_rest(engine, ops, k, 0, rest_taken)
                third_part(engine, ops, k - 1, 0, ready)
            third_part(engine, ops, places[-1], 0, ready)

        def wait_alone(engine, semaphore, value):
            engine.wait_ge(semaphore, value)
            engine.sem_inc(waited, 1)

        x_order = [BLOCKS // 2 - 1] + list(range(BLOCKS // 2 - 1))

        block = ctx.enter_context(nc.Block())

        @block.sync
        def _(sp):
            sp.dma_start(dst_all[:, :], dst_t).then_inc(dst_loaded, 16)
            sp.dma_start(be_bc[:, :], be[0:1, :].to_broadcast([P, D])).then_inc(be_loaded, 16)
            x_blocks = x_pad.rearrange("(b p) d -> p b d", p=P)
            for k in x_order:
                sp.dma_start(x_now[:, 2 * k:2 * k + 2, :], x_blocks[:, 2 * k:2 * k + 2, :]).then_inc(x_loaded[k], 16)
            sp.dma_start(w_all[:, :], w_t).then_inc(w_loaded, 16)
            sp.dma_start(src_all[:, :], src_t).then_inc(src_loaded, 16)

            def write_block(b, part=slice(0, D)):
                for a, z, n in real_rows(b):
                    sp.dma_start(table[n:n + z - a, part], rows[a:z, STEP // 2 + b, part]).then_inc(table_written, 16)

            for k, b in enumerate(ORDER):
                sp.wait_ge(staged, k + 1)
                write_block(b)
            sp.dma_start(We_bc[:, :], We[0:1, :].to_broadcast([P, D])).then_inc(We_loaded, 16)
            sp.dma_start(src_bc[:, :, :].rearrange("q b p -> q (b p)"),
                         src_late.to_broadcast([P, (BLOCKS - 1) * P])).then_inc(src_bc_loaded, 16)
            with sp.Fori(0, L) as l:
                wait_alone(sp, params_free, 3 * l + 3)
                sp.dma_start(eps_cur[:, :], eps[bass.ds(l, 1), :].to_broadcast([P, 1])).then_inc(params_loaded, 16)
                sp.dma_start(vec[:, :, :], vectors[bass.ds(l, 1), :, :, :].rearrange("o p v c -> p (o v) c")).then_inc(params_loaded, 16)
                sp.dma_start(W1_sb[:, :, :], W1[bass.ds(l, 1), :, :].rearrange("o (c p) d -> p (o c) d", p=P)).then_inc(params_loaded, 16)
                sp.dma_start(W2_sb[:, :, :], W2[bass.ds(l, 1), :, :].rearrange("o (c p) d -> p (o c) d", p=P)).then_inc(params_loaded, 16)
                sp.dma_start(b2_bc[:, :], b2[bass.ds(l, 1), :].to_broadcast([P, D])).then_inc(params_loaded, 16)
                sp.dma_start(be_bc[:, :], be[bass.ds(l + 1, 1), :].to_broadcast([P, D])).then_inc(params_loaded, 16)
                sp.dma_start(We_bc[:, :], We[bass.ds(l + 1, 1), :].to_broadcast([P, D])).then_inc(params_loaded, 16)
                with sp.If(l == L - 1):
                    sp.wait_ge(bn_ready, 2 * L)
                    for k in x_order:
                        sp.dma_start(rows[:, x_slot(2 * k):x_slot(2 * k) + 2, :],
                                     x_blocks[:, 2 * k:2 * k + 2, :]).then_inc(x_reloaded[k], 16)
                    for k, b in enumerate(ORDER):
                        sp.wait_ge(ln_ready, k + 1)
                        for a, z, n in real_rows(b):
                            sp.dma_start(out[n:n + z - a, :], rows[a:z, b, :]).then_inc(out_written, 16)
                with sp.Else():
                    for k, b in enumerate(ORDER[:-1]):
                        sp.wait_ge(staged, BLOCKS * (l + 1) + k + 1)
                        write_block(b)
                    sp.wait_ge(half_staged, l + 1)
                    write_block(ORDER[-1], HALVES[0])
                    sp.wait_ge(staged, BLOCKS * (l + 2))
                    write_block(ORDER[-1], HALVES[1])
                sp.nop()
            sp.wait_ge(table_written, WRITES + (L - 1) * MORE_WRITES)
            sp.wait_ge(out_written, WRITES)

        @block.gpsimd
        def _(pool):
            nc.gpsimd.iota(cols[:, :], [[1, 2 * P]], base=0, channel_multiplier=0,
                           allow_small_or_imprecise_dtypes=True)
            nc.gpsimd.iota(part[:, :], [[0, 1]], base=0, channel_multiplier=1,
                           allow_small_or_imprecise_dtypes=True)
            nc.gpsimd.iota(node[:, :], [[P, BLOCKS]], base=-MARGIN, channel_multiplier=1,
                           allow_small_or_imprecise_dtypes=True)
            nc.gpsimd.iota(starts[:, :], [[WIN // 2, T_PAD // RUN], [0, RUN]], base=0, channel_multiplier=0,
                           allow_small_or_imprecise_dtypes=True).then_inc(iotas, 1)
            pool.wait_ge(iotas, 1)
            first = T - SHORT + SPLIT
            nc.gpsimd.iota(starts[:, first:T], [[0, T - first]], base=(T - SHORT) // RUN * (WIN // 2) + WIN // 2,
                           channel_multiplier=0, allow_small_or_imprecise_dtypes=True).then_inc(iotas, 1)
            nc.gpsimd.memset(hT[:, :, 0:GUARD], 0.0)
            nc.gpsimd.memset(carry[:, :], 0.0).then_inc(cleared, 1)

            def gather(quads, l, i):
                for q, quad in enumerate(quads):
                    if q % 4 == 0:
                        pool.wait_ge(cols_ready, 2 * BLOCKS * l + 2 * i + q // 4 + 1)
                    if q == BLOCKS // 4:
                        wait_alone(pool, split[3], BLOCKS * (l + 1))
                    wait_alone(pool, quad_summed[q], BLOCKS * l + i + 1)
                    for slot, tile, _ in quad:
                        if tile == GATHERED:
                            continue
                        nc.gpsimd.indirect_dma_start(
                            rows[:, slot, :], None, table[:, :],
                            bass.IndirectOffsetOnAxis(src_cur[:, tile:tile + 1], 0)).then_inc(landed[q], 16)

            split_table(pool, nc.gpsimd, range(EARLY), early_split[0], early_split[1])
            pool.wait_ge(early_split[1], EARLY)
            pool.wait_ge(flag_ready, 1)
            slow = pool.value_load(flag[0:1, 0:1], min_val=0, max_val=1)
            with pool.Fori(0, L) as l:
                pool.wait_ge(table_written, MORE_WRITES * l + WRITES)
                wait_alone(pool, x_updated, BLOCKS * l + 1)
                with pool.If(slow == 0):
                    with pool.Fori(0, BLOCKS - 1) as i:
                        gather(FULL, l, i)
                    gather(FINAL, l, BLOCKS - 1)
                with pool.Else():
                    with pool.Fori(0, T) as t:
                        wait_alone(pool, slow_cols, T * l + t + 1)
                        nc.gpsimd.indirect_dma_start(
                            rows[:, 0, :], None, table[:, :],
                            bass.IndirectOffsetOnAxis(src_one[:, 0:1], 0)).then_inc(slow_landed, 16)
                pool.nop()

        @block.scalar
        def _(act):

            def move_parts(step, h):
                nc.scalar.copy(w_parts_cur[:, h * PAIR:(h + 1) * PAIR, :],
                               w_parts[:, bass.ds(STEP * step + h * PAIR, PAIR), :]).then_inc(w_cols_ready[h], 1)

            for k in range(BLOCKS):
                act.wait_ge(staged, k + 1)
                first_part(k, 0)
                if 0 < k <= EARLY:
                    second_part(act, k - 1, 0, early_split[0])

            def move_cols(step, h):
                nc.scalar.copy(src_cur[:, h * PAIR:(h + 1) * PAIR], src_all[:, bass.ds(STEP * step + h * PAIR, PAIR)])
                nc.scalar.copy(negw_cur[:, h * PAIR:(h + 1) * PAIR],
                               negw_all[:, bass.ds(STEP * step + h * PAIR, PAIR)]).then_inc(cols_ready, 1)

            act.wait_ge(src_loaded, 16)
            act.wait_ge(negw_ready, 1)
            move_cols(0, 0)
            move_cols(0, 1)
            act.wait_ge(We_loaded, 16)
            nc.scalar.copy(We_ps[:, :], We_bc[:, :]).then_inc(We_ready, 1)
            for k in range(EARLY, BLOCKS):
                second_part(act, k, 0, split[1])
            act.wait_ge(w_parts_ready, 1)
            move_parts(0, 0)
            move_parts(0, 1)

            def copy_w(n, to):
                for h in range(2):
                    act.wait_ge(w_summed[h], n + 2)
                    nc.scalar.mul(to[:, h, :], y_ps[1 + h][:, 0:3], -1.0).then_inc(w_copied, 1)

            copy_w(0, pair_w)
            move_parts(BLOCKS - 1, 0)
            move_parts(BLOCKS - 1, 1)
            act.wait_ge(w_placed, 1)
            nc.scalar.activation(w_sum[:, 0:1], y_ps[1][:, 8:9], ACT.Copy, scale=ok[:, 0:1]).then_inc(w_sum_ready, 1)
            copy_w(1, last_pair_w)
            for loaded in x_loaded:
                act.wait_ge(loaded, 16)
            act.wait_ge(w_sum_ready, 1)

            def next_w(i):
                act.wait_ge(w_copied, 2 * i + 4)
                nc.scalar.copy(pair_w[:, 2, :], pair_w[:, 1, :]).then_inc(w_shifted, 1)
                wait_alone(act, w_shifted, i + 1)
                with act.If(i == BLOCKS - 2):
                    for h in range(2):
                        act.wait_ge(w_summed[h], BLOCKS + 2)
                        nc.scalar.copy(pair_w[:, h, :], last_pair_w[:, h, :]).then_inc(w_copied, 1)
                with act.Else():
                    copy_w(i + 2, pair_w)

            def keep_w(i):
                act.wait_ge(w_placed, i + 2)
                nc.scalar.copy(w_sum[:, bass.ds(i + 1, 1)], y_ps[1][:, 8:9]).then_inc(w_sum_ready, 1)
                wait_alone(act, w_sum_ready, i + 2)

            def scale_u(n, i):
                act.wait_ge(block_summed, n + 1)
                nc.scalar.copy(w_sum_cur[:, :], w_sum[:, bass.ds(i, 1)])
                nc.scalar.activation(u[:, :], x_now[:, bass.ds(i, 1), :].rearrange("p o d -> p (o d)"),
                                     ACT.Identity, scale=eps1[:, 0:1]).then_inc(u_scaled, 1)

            def copy_pair(h, n, summed, value):
                act.wait_ge(block_summed, n + 1)
                act.wait_ge(summed, value)
                nc.scalar.copy(pair_sb[:, h, :], pair_ps[h][:, :]).then_inc(pair_copied[h], 1)

            def finish_block(n, i):
                act.wait_ge(block_summed, n + 2)
                act.wait_ge(h_summed, n + 1)
                nc.scalar.copy(uT[:, :, :], uT_ps[:, :, :]).then_inc(uT_copied, 1)

            def finish_h(n, i):
                act.wait_ge(h_summed, n + 2)
                for c in range(C):
                    last = nc.scalar.activation(
                        hT[:, c:c + 1, bass.ds(P * i + GUARD - MARGIN, P)].rearrange("p o n -> p (o n)"),
                        h_ps[:, c, :], ACT.Identity, bias=vec[:, 0, c:c + 1])
                last.then_inc(h_copied, 1)

            act.wait_ge(flag_ready, 1)
            slow = act.value_load(flag[0:1, 0:1], min_val=0, max_val=1)
            with act.Fori(0, L) as l:
                act.wait_ge(params_loaded, PARAMS * (l + 1))
                nc.scalar.activation(eps1[:, :], eps_cur[:, :], ACT.Identity, bias=1.0).then_inc(eps_ready, 1)
                wait_alone(act, eps_ready, l + 1)
                with act.If(slow == 0):
                    scale_u(BLOCKS * l, 0)
                    with act.Fori(0, BLOCKS - 1) as i:
                        n = BLOCKS * l + i
                        with act.If(l == 0):
                            move_parts(i + 1, 0)
                            move_parts(i + 1, 1)
                        act.wait_ge(v_ready[3], BLOCKS * l + i + 1)
                        move_cols(i + 1, 0)
                        copy_pair(0, n, quad_summed[3], BLOCKS * l + i + 2)
                        act.wait_ge(tile_gathered, (BLOCKS - 1) * l + i + 2)
                        nc.scalar.copy(rows[:, GATHERED, :], y_ps[0][:, :]).then_inc(tile_moved, 1)
                        act.wait_ge(v_ready[7], BLOCKS * l + i + 1)
                        move_cols(i + 1, 1)
                        with act.If(l == 0):
                            next_w(i)
                        copy_pair(1, n, quad_summed[7], BLOCKS * l + i + 2)
                        finish_block(n, i)
                        nc.scalar.copy(carry[3 * P // 4:P, :], pair_sb[3 * P // 4:P, 1, :]).then_inc(carry_copied, 1)
                        with act.If(l == 0):
                            keep_w(i)
                        scale_u(n + 1, i + 1)
                        finish_h(n, i)
                    i = BLOCKS - 1
                    n = BLOCKS * l + i
                    copy_pair(0, n, quad_summed[3], BLOCKS * l + i + 2)
                    copy_pair(1, n, quad_summed[7], BLOCKS * l + i + 2)
                    finish_block(n, i)
                    act.wait_ge(h_copied, n + 1)
                    nc.scalar.activation(unread[:, :], eps_col[:, :], ACT.Sqrt)
                with act.Else():
                    with act.Fori(0, T) as t:
                        act.wait_ge(slow_done, T * l + t + 1)
                        nc.scalar.copy(src_one[:, :], src_all[:, bass.ds(t, 1)])
                        nc.scalar.copy(row_one[:, :], row_all[:, bass.ds(t, 1)])
                        nc.scalar.copy(negw_one[:, :], negw_all[:, bass.ds(t, 1)]).then_inc(slow_cols, 1)
                    with act.Fori(0, BLOCKS) as i:
                        n = BLOCKS * l + i
                        scale_u(n, i)
                        finish_block(n, i)
                        finish_h(n, i)

                def std_of(g):
                    f = GROUPS[g]
                    act.wait_ge(var_ready, C * l + f.stop)
                    nc.scalar.activation(std[:, f], mv[:, f, 1], ACT.Sqrt, bias=eps_col[:, 0:1]).then_inc(std_ready, 1)

                def bn_relu(b, c):
                    at = GUARD - MARGIN + P * b
                    nc.scalar.activation(hT[:, c, at:at + P], hT[:, c, at:at + P], ACT.Relu,
                                         bias=bn_bias[:, c:c + 1], scale=bn_scale[:, c:c + 1]).then_inc(hr_ready, 1)

                def bn_relus(m):
                    for k, (place, c) in enumerate(HR_ORDER):
                        if place == m or m == 0 and place < AHEAD:
                            if k == 0:
                                std_of(0)
                                act.wait_ge(bn_ready, 2 * l + 1)
                            if k == FEW * (AHEAD - 1):
                                std_of(1)
                            if k == FEW * AHEAD:
                                act.wait_ge(bn_ready, 2 * l + 2)
                            bn_relu(ORDER[place], c)

                def prepare_layer():
                    nc.scalar.copy(We_ps[:, :], We_bc[:, :]).then_inc(We_ready, 1)
                    move_cols(0, 0)
                    move_cols(0, 1)

                relu_places = [0] + list(range(AHEAD, BLOCKS))
                with act.If(l == L - 1):
                    def ln_std_of(k):
                        b = ORDER[k]
                        act.wait_ge(ln_var_ready, k + 1)
                        nc.scalar.activation(ln_std[:, b:b + 1], ln_mv[:, b, 1:2], ACT.Sqrt,
                                             bias=eps_col[:, 0:1]).then_inc(ln_std_ready, 1)

                    for m in relu_places:
                        bn_relus(m)
                        if m >= LAG:
                            ln_std_of(m - LAG)
                    for k in range(BLOCKS - LAG, BLOCKS):
                        ln_std_of(k)
                with act.Else():
                    def keep_block(k):
                        b = ORDER[k]
                        act.wait_ge(y_added, BLOCKS * l + k + 1)
                        nc.scalar.activation(x_now[:, b, :], y_stage(b), ACT.Relu,
                                             scale=mask[:, b:b + 1]).then_inc(x_updated, 1)
                        act.wait_ge(staged, BLOCKS * (l + 1) + k + 1)
                        first_part(k, BLOCKS * (l + 1))
                        if k:
                            second_part(act, k - 1, BLOCKS * (l + 1), split[1])

                    for m in relu_places:
                        bn_relus(m)
                        if m == LAG:
                            prepare_layer()
                        if m >= LAG:
                            keep_block(m - LAG)
                    for k in range(BLOCKS - LAG, BLOCKS):
                        keep_block(k)
                    second_part(act, BLOCKS - 1, BLOCKS * (l + 1), split[1])
                    wait_alone(act, x_updated, BLOCKS * (l + 1) + 1)
                act.sem_inc(params_free, 1)

        @block.vector
        def _(dve):
            done = [0]

            def then_wait(ins):
                done[0] += 1
                ins.then_inc(prep, 1)
                dve.wait_ge(prep, done[0])

            nc.vector.memset(ones[:, :], 1.0)
            nc.vector.memset(eps_col[:, :], EPS)
            nc.vector.memset(pair_w[:, :, :], 0.0)
            nc.vector.memset(w_sum[:, :], 0.0)
            nc.vector.memset(w_parts[:, T_PAD:, :], 0.0)
            for s in w_summed + quad_summed + pair_copied + [carry_copied, tile_gathered, block_summed, uT_copied, h_summed,
                                                             h_copied, slow_done, x_updated]:
                dve.sem_inc(s, 1)
            dve.wait_ge(dst_loaded, 16)
            then_wait(nc.vector.tensor_scalar(row_all[:, :], dst_all[:, :], float(MARGIN), None, ALU.add))
            dve.wait_ge(iotas, 2)
            then_wait(nc.vector.tensor_tensor(local_all[:, :], row_all[:, :], starts[:, :], ALU.subtract))
            then_wait(nc.vector.tensor_scalar(rest[:, :], local_all[:, :], 0.0, None, ALU.is_lt))
            nc.vector.scalar_tensor_tensor(rest[:, :], local_all[:, :], float(WIN - 1), rest[:, :],
                                           ALU.is_gt, ALU.add, accum_out=bad[:, :]).then_inc(bad_counted, 1)
            dve.wait_ge(bad_summed, 1)
            then_wait(nc.vector.tensor_scalar(ok[:, :], y_ps[2][:, BLOCKS:BLOCKS + 1], 0.0, None, ALU.is_equal))
            nc.vector.tensor_scalar(flag[:, :], ok[0:1, 0:1], 0.0, None, ALU.is_equal).then_inc(flag_ready, 1)

            def make_onehot(i, h, to, ready, tiles=PAIR):
                nc.vector.tensor_tensor(
                    to[:, h, 0:tiles, :], cols[:, 0:WIN].unsqueeze(1).to_broadcast([P, tiles, WIN]),
                    local_all[:, bass.ds(STEP * i + h * PAIR, tiles)].unsqueeze(2).to_broadcast([P, tiles, WIN]),
                    ALU.is_equal).then_inc(ready, 1)

            dve.wait_ge(be_loaded, 16)
            for b in ORDER:
                dve.wait_ge(x_loaded[b // 2], 16)
                nc.vector.tensor_tensor(table_stage(b), x_now[:, b, :], be_bc[:, :], ALU.add).then_inc(staged, 1)
            dve.wait_ge(w_loaded, 16)
            then_wait(nc.vector.tensor_scalar(negw_all[:, :], w_all[:, :], -1.0, None, ALU.mult))
            dve.sem_inc(negw_ready, 1)
            left = negw_all
            for k in range(3):
                then_wait(nc.vector.tensor_copy(w_parts[:, 0:T_PAD, k], left[:, :]))
                if k < 2:
                    then_wait(nc.vector.tensor_tensor(rest[:, :], left[:, :], w_parts[:, 0:T_PAD, k], ALU.subtract))
                    left = rest
            dve.sem_inc(w_parts_ready, 1)
            nc.vector.tensor_scalar(ident[:, :], cols[:, 0:P], part[:, 0:1], None, ALU.is_equal)
            nc.vector.tensor_scalar(mask_lo[:, :], node[:, :], 0.0, None, ALU.is_ge)
            then_wait(nc.vector.tensor_scalar(upper[:, :], part[:, :], float(WIN), -float(WIN - 2 * MARGIN),
                                              ALU.is_ge, ALU.mult))
            nc.vector.scalar_tensor_tensor(mask[:, :], node[:, :], float(N), mask_lo[:, :], ALU.is_lt, ALU.mult)
            then_wait(nc.vector.scalar_tensor_tensor(target[:, :], part[:, :], float(WIN), upper[:, :],
                                                     ALU.add, ALU.add))
            nc.vector.tensor_scalar(place[:, :], cols[:, :], target[:, 0:1], None,
                                    ALU.is_equal).then_inc(masks_ready, 1)
            dve.wait_ge(early_split[1], EARLY)
            dve.sem_inc(split[1], EARLY)
            dve.sem_inc(split[3], EARLY)
            split_table(dve, nc.vector, range(EARLY, BLOCKS), split[1], split[3])
            dve.wait_ge(staged, BLOCKS)
            dve.wait_ge(We_ready, 1)
            dve.sem_inc(params_free, 3)

            def w_onehots(n, i):
                for h in range(2):
                    dve.wait_ge(w_summed[h], n + 1)
                    make_onehot(i, h, onehot_bf, w_onehot_ready[h])

            w_onehots(0, 0)
            w_onehots(1, BLOCKS - 1)

            def messages(quads, q, l, i):
                quad = quads[q]
                dve.wait_ge(landed[q], landed_count(q, l, i) + 16 * sum(tile != GATHERED for _, tile, _ in quad))
                for slot, tile, _ in quad:
                    if tile == GATHERED:
                        dve.wait_ge(tile_moved, (BLOCKS - 1) * l + i + 1)
                    last = nc.vector.scalar_tensor_tensor(rows[:, slot, :], We_ps[:, :], negw_cur[:, tile:tile + 1],
                                                          rows[:, slot, :], ALU.mult, ALU.max)
                last.then_inc(v_ready[q], 1)

            def finish_u(n, ready):
                dve.wait_ge(u_scaled, n + 1)
                return nc.vector.scalar_tensor_tensor(u[:, :], We_ps[:, :], w_sum_cur[:, 0:1], u[:, :],
                                                      ALU.mult, ALU.add).then_inc(ready, 1)

            def block_stats(n, i):
                dve.wait_ge(h_copied, n + 1)
                for c in range(C):
                    last = nc.vector.bn_stats(stats[:, c, bass.ds(i, 1), :].rearrange("p o s -> p (o s)"),
                                              hT[:, c:c + 1, bass.ds(P * i, P)].rearrange("p o n -> p (o n)"))
                return last

            def late_stats(slot, a, z):
                for c in range(C):
                    last = nc.vector.bn_stats(stats[:, c, slot, :], hT[:, c, a:z])
                return last

            def mean_and_variance(l, c):
                wait_alone(dve, stats_done, C * l + c + 1)
                nc.vector.bn_aggr(mv[:, c, :], stats[:, c, 2:BLOCKS + 2, :].rearrange("p s k -> p (s k)"),
                                  ).then_inc(var_ready, 1)

            def bn_scales(l, g):
                f = GROUPS[g]
                dve.wait_ge(std_ready, 2 * l + g + 1)
                nc.vector.reciprocal(rstd[:, f], std[:, f]).then_inc(bn_chain, 1)
                dve.wait_ge(bn_chain, 3 * (2 * l + g) + 1)
                dve.wait_ge(params_loaded, PARAMS * (l + 1))
                nc.vector.tensor_tensor(bn_scale[:, f], rstd[:, f], vec[:, 1, f], ALU.mult).then_inc(bn_chain, 1)
                dve.wait_ge(bn_chain, 3 * (2 * l + g) + 2)
                nc.vector.tensor_tensor(bn_shift[:, f], mv[:, f, 0], bn_scale[:, f], ALU.mult).then_inc(bn_chain, 1)
                dve.wait_ge(bn_chain, 3 * (2 * l + g) + 3)
                nc.vector.tensor_tensor(bn_bias[:, f], vec[:, 2, f], bn_shift[:, f], ALU.subtract).then_inc(bn_ready, 1)

            def edge_step(quads, l, i):
                n = BLOCKS * l + i
                if quads is FULL:
                    dve.wait_ge(tile_gathered, (BLOCKS - 1) * l + i + 1)
                    nc.vector.tensor_tensor(
                        src_onehot[:, :, :], node[:, :].unsqueeze(2).to_broadcast([P, BLOCKS, P]),
                        src_bc[:, bass.ds(i, 1), :].to_broadcast([P, BLOCKS, P]),
                        ALU.is_equal).then_inc(src_onehot_ready, 1)
                for h in range(2):
                    dve.wait_ge(quad_summed[4 * h + 3], BLOCKS * l + i + 1)
                    make_onehot(i, h, onehot, onehot_ready, SHORT if quads is FINAL and h == 1 else PAIR)
                    dve.wait_ge(cols_ready, 2 * BLOCKS * l + 2 * i + h + 1)
                    for q in range(4 * h, 4 * h + 4):
                        messages(quads, q, l, i)
                        if q == 2:
                            finish_u(n, u_ready)
                        if q == 5 and quads is FULL:
                            block_stats(n, i)
                            with dve.If(l == 0):
                                w_onehots(i + 2, i + 1)
                if quads is FINAL:
                    block_stats(n, i)
                    late_stats(BLOCKS, GUARD + (BLOCKS - 2) * P, GUARD - MARGIN + (BLOCKS - 1) * P)

            dve.wait_ge(src_bc_loaded, 16)
            dve.wait_ge(flag_ready, 1)
            slow = dve.value_load(flag[0:1, 0:1], min_val=0, max_val=1)
            with dve.Fori(0, L) as l:
                dve.wait_ge(x_updated, BLOCKS * l + 1)
                dve.wait_ge(cleared, 1)
                nc.vector.memset(carry[3 * P // 4:P, :], 0.0).then_inc(carry_cleared, 1)
                wait_alone(dve, We_ready, l + 1)
                with dve.If(slow == 0):
                    with dve.Fori(0, BLOCKS - 1) as i:
                        edge_step(FULL, l, i)
                    edge_step(FINAL, l, BLOCKS - 1)
                    for c in range(C):
                        if c < C - 1:
                            dve.wait_ge(h_part_summed, (C - 1) * l + c + 1)
                        else:
                            dve.wait_ge(h_summed, BLOCKS * l + BLOCKS + 1)
                        nc.vector.tensor_scalar(
                            hT[:, c, GUARD - MARGIN + (BLOCKS - 1) * P:GUARD - MARGIN + BLOCKS * P], last_h(c),
                            vec[:, 0, c:c + 1], None, ALU.add).then_inc(h_part_copied if c < C - 1 else h_copied, 1)
                        if c < C - 1:
                            dve.wait_ge(h_part_copied, (C - 1) * l + c + 1)
                        else:
                            dve.wait_ge(h_copied, BLOCKS * l + BLOCKS + 1)
                        if c == FEW:
                            bn_scales(l, 0)
                        nc.vector.bn_stats(stats[:, c, BLOCKS + 1, :],
                                           hT[:, c, GUARD - MARGIN + (BLOCKS - 1) * P:GUARD + N]).then_inc(stats_done, 1)
                        mean_and_variance(l, c)
                    bn_scales(l, 1)
                with dve.Else():
                    sums = rows[:, SLOW_SUMS:SLOW_SUMS + BLOCKS, :]
                    dve.wait_ge(split[3], BLOCKS * (l + 1))
                    dve.wait_ge(table_written, MORE_WRITES * l + WRITES)
                    nc.vector.memset(sums, 0.0).then_inc(slow_cleared, 1)
                    wait_alone(dve, slow_cleared, l + 1)
                    with dve.Fori(0, T) as t:
                        k0 = (2 + BLOCKS) * (T * l + t)
                        dve.wait_ge(slow_landed, 16 * (T * l + t + 1))
                        nc.vector.scalar_tensor_tensor(rows[:, 0, :], We_ps[:, :], negw_one[:, 0:1], rows[:, 0, :],
                                                       ALU.mult, ALU.max).then_inc(slow_chain, 1)
                        dve.wait_ge(slow_chain, k0 + 1)
                        nc.vector.scalar_tensor_tensor(rows[:, 1, :], We_ps[:, :], negw_one[:, 0:1], rows[:, 0, :],
                                                       ALU.mult, ALU.subtract).then_inc(slow_chain, 1)
                        for b in range(BLOCKS):
                            m = BLOCKS * (T * l + t) + b
                            dve.wait_ge(slow_chain, k0 + 2 + b)
                            nc.vector.tensor_scalar(onehot_block[:, :], cols[:, 0:P], float(P * b), row_one[:, 0:1],
                                                    ALU.add, ALU.is_equal).then_inc(slow_onehot, 1)
                            dve.wait_ge(slow_summed, m + 1)
                            nc.vector.tensor_tensor(sums[:, b, :], sums[:, b, :], y_ps[0][:, :],
                                                    ALU.subtract).then_inc(slow_chain, 1)
                        dve.wait_ge(slow_chain, k0 + 2 + BLOCKS)
                        dve.sem_inc(slow_done, 1)
                    with dve.Fori(0, BLOCKS) as i:
                        n = BLOCKS * l + i
                        finish_u(n, slow_u)
                        dve.wait_ge(slow_u, n + 1)
                        nc.vector.tensor_tensor(
                            u[:, :], rows[:, bass.ds(SLOW_SUMS + i, 1), :].rearrange("p o d -> p (o d)"), u[:, :],
                            ALU.add).then_inc(u_ready, 1)
                        block_stats(n, i)
                    dve.wait_ge(h_copied, BLOCKS * l + BLOCKS + 1)
                    late_stats(BLOCKS, GUARD + (BLOCKS - 2) * P, GUARD - MARGIN + (BLOCKS - 1) * P)
                    late_stats(BLOCKS + 1, GUARD - MARGIN + (BLOCKS - 1) * P, GUARD + N).then_inc(stats_done, C)
                    dve.sem_inc(h_part_copied, C - 1)
                    for c in range(C):
                        mean_and_variance(l, c)
                    bn_scales(l, 0)
                    bn_scales(l, 1)

                def add_b2(k, b):
                    dve.wait_ge(y_summed, BLOCKS * l + k + 1)
                    nc.vector.tensor_tensor(y_stage(b), y_ps[k % 3][:, :], b2_bc[:, :], ALU.add).then_inc(y_added, 1)
                    dve.wait_ge(y_added, BLOCKS * l + k + 1)

                def add_b2_half(b, h):
                    summed, added = (half_summed, half_added) if h == 0 else (y_summed, y_added)
                    count = l + 1 if h == 0 else BLOCKS * (l + 1)
                    dve.wait_ge(summed, count)
                    nc.vector.tensor_tensor(y_stage(b)[:, HALVES[h]], y_half(h), b2_bc[:, HALVES[h]],
                                            ALU.add).then_inc(added, 1)
                    dve.wait_ge(added, count)

                with dve.If(l == L - 1):
                    def ln_second(k, b):
                        dve.wait_ge(ln_std_ready, k + 1)
                        nc.vector.reciprocal(ln_rstd[:, b:b + 1], ln_std[:, b:b + 1]).then_inc(ln_scaled, 1)
                        dve.wait_ge(ln_scaled, k + 1)
                        nc.vector.tensor_scalar(y_stage(b), table_stage(b), ln_mv[:, b, 0:1], ln_rstd[:, b:b + 1],
                                                ALU.subtract, ALU.mult).then_inc(ln_ready, 1)

                    for k, b in enumerate(ORDER):
                        if k < BLOCKS - 1:
                            add_b2(k, b)
                        else:
                            add_b2_half(b, 0)
                            add_b2_half(b, 1)
                        dve.wait_ge(x_reloaded[b // 2], 16)
                        nc.vector.scalar_tensor_tensor(table_stage(b), y_stage(b), 0.0, rows[:, x_slot(b), :],
                                                       ALU.max, ALU.add).then_inc(ln_chain, 1)
                        dve.wait_ge(ln_chain, 2 * k + 1)
                        nc.vector.bn_stats(ln_stats[:, b, :], table_stage(b)).then_inc(ln_chain, 1)
                        dve.wait_ge(ln_chain, 2 * k + 2)
                        nc.vector.bn_aggr(ln_mv[:, b, :], ln_stats[:, b, :]).then_inc(ln_var_ready, 1)
                        if k:
                            ln_second(k - 1, ORDER[k - 1])
                    ln_second(BLOCKS - 1, ORDER[-1])
                with dve.Else():
                    for k, b in enumerate(ORDER):
                        if k < BLOCKS - 1:
                            add_b2(k, b)
                            nc.vector.scalar_tensor_tensor(table_stage(b), y_stage(b), 0.0, be_bc[:, :],
                                                           ALU.max, ALU.add).then_inc(staged, 1)
                        else:
                            for h, f in enumerate(HALVES):
                                add_b2_half(b, h)
                                nc.vector.scalar_tensor_tensor(
                                    table_stage(b)[:, f], y_stage(b)[:, f], 0.0, be_bc[:, f],
                                    ALU.max, ALU.add).then_inc(staged if h else half_staged, 1)
                        if k:
                            take_rest(dve, nc.vector, k - 1, BLOCKS * (l + 1), split[1])
                        if k > 1:
                            third_part(dve, nc.vector, k - 2, BLOCKS * (l + 1), split[3])
                    take_rest(dve, nc.vector, BLOCKS - 1, BLOCKS * (l + 1), split[1])
                    for k in (BLOCKS - 2, BLOCKS - 1):
                        third_part(dve, nc.vector, k, BLOCKS * (l + 1), split[3])
                    wait_alone(dve, staged, BLOCKS * (l + 2))
                dve.sem_inc(params_free, 1)

        @block.tensor
        def _(pe):
            pe.wait_ge(bad_counted, 1)
            nc.tensor.matmul(y_ps[2][:, BLOCKS:BLOCKS + 1], ones[:, :], bad[:, :],
                             start=True, stop=True).then_inc(bad_summed, 1)
            def sum_w(quads, n, kept=None):
                if kept is not None:
                    pe.wait_ge(w_sum_ready, kept)
                for h in range(2):
                    pe.wait_ge(w_onehot_ready[h], n + 1)
                    pe.wait_ge(w_cols_ready[h], n + 1)
                    tiles, firsts, lasts = tiles_of(quads, h)
                    for t in tiles:
                        _, tile, win = t
                        last = nc.tensor.matmul(y_ps[1 + h][WIN * win:WIN * (win + 1), 0:3],
                                                onehot_bf[:, h, tile - h * PAIR, :], w_parts_cur[:, tile, :],
                                                start=t in firsts, stop=t in lasts)
                    last.then_inc(w_summed[h], 1)

            placements = [(k, m, at) for k in range(3) for m, at in enumerate((WIN, 0, P))]

            def place_w(n, some):
                pe.wait_ge(w_copied, 2 * n + 2)
                for k, m, at in some:
                    last = nc.tensor.matmul(y_ps[1][:, 8:9], place[:, at:at + P], pair_w[:, m, k:k + 1],
                                            start=(k, m) == (0, 0), stop=(k, m) == (2, 2))
                if some[-1] == placements[-1]:
                    last.then_inc(w_placed, 1)

            sum_w(FULL, 0)
            pe.wait_ge(masks_ready, 1)
            pe.wait_ge(flag_ready, 1)
            place_w(0, placements)
            sum_w(FINAL, 1, 1)

            def sum_pair(quads, h, l, i):
                pe.wait_ge(pair_copied[h], BLOCKS * l + i + 1)
                pe.wait_ge(onehot_ready, 2 * BLOCKS * l + 2 * i + h + 1)
                _, firsts, lasts = tiles_of(quads, h)
                for q in range(4 * h, 4 * h + 4):
                    pe.wait_ge(v_ready[q], BLOCKS * l + i + 1)
                    for t in quads[q]:
                        slot, tile, win = t
                        last = nc.tensor.matmul(pair_ps[h][WIN * win:WIN * (win + 1), :],
                                                onehot[:, h, tile - h * PAIR, :], rows[:, slot, :],
                                                start=t in firsts, stop=t in lasts)
                    last.then_inc(quad_summed[q], 1)
                    if quads is FULL and SHARE[q]:
                        gather_share(q, l, i)
                    if quads is FULL and q == 6:
                        with pe.If(l == 0):
                            sum_w(FULL, i + 2, i + 1)
                    if q == 2:
                        open_block(BLOCKS * l + i, l, i, True)
                    if q == 4:
                        add_first_pair(BLOCKS * l + i)

            def gather_share(q, l, i):
                products = [(part, b) for part in range(3) for b in range(BLOCKS)]
                start = sum(SHARE[:q])
                if start == 0:
                    pe.wait_ge(src_onehot_ready, (BLOCKS - 1) * l + i + 1)
                    pe.wait_ge(early_split[1], EARLY)
                    pe.wait_ge(split[3], BLOCKS * (l + 1))
                for m in range(start, start + SHARE[q]):
                    part, b = products[m]
                    last = nc.tensor.matmul(y_ps[0][:, :], src_onehot[:, b, :], table_parts[:, part, b, :],
                                            start=(m == 0), stop=(m == len(products) - 1))
                if start + SHARE[q] == len(products):
                    last.then_inc(tile_gathered, 1)

            def open_block(n, l, i, pairs):
                pe.wait_ge(u_ready, n + 1)
                pe.wait_ge(uT_copied, n + 1)
                chunks = [slice(c * P, (c + 1) * P) for c in range(C)]
                for c, f in enumerate(chunks):
                    last = nc.tensor.matmul(uT_ps[:, c, :], u[:, f], ident[:, :], start=(c == 0),
                                            stop=not pairs, skip_group_check=True)
                if not pairs:
                    last.then_inc(block_summed, 1)
                    return
                pe.wait_ge(carry_cleared, l + 1)
                pe.wait_ge(carry_copied, (BLOCKS - 1) * l + i + 1)
                for c, f in enumerate(chunks):
                    nc.tensor.matmul(uT_ps[:, c, 0:PLACED - WIN], carry[:, f], place[:, P:WIN + PLACED],
                                     start=False, stop=False, skip_group_check=True)

            def add_first_pair(n):
                pe.wait_ge(pair_copied[0], n + 2)
                for c in range(C):
                    f = slice(c * P, (c + 1) * P)
                    nc.tensor.matmul(uT_ps[:, c, 0:PLACED], pair_sb[:, 0, f], place[:, WIN:WIN + PLACED],
                                     start=False, stop=False, skip_group_check=True)

            def close_block(n):
                pe.wait_ge(pair_copied[1], n + 2)
                for c in range(C):
                    last = nc.tensor.matmul(uT_ps[:, c, WIN:P], pair_sb[:, 1, c * P:(c + 1) * P],
                                            place[:, WIN:P], start=False, stop=True, skip_group_check=True)
                last.then_inc(block_summed, 1)

            def product_h(n, l, apart=False):
                pe.wait_ge(params_loaded, PARAMS * (l + 1))
                pe.wait_ge(uT_copied, n + 2)
                pe.wait_ge(h_copied, n + 1)
                for c in range(C):
                    for k in range(C):
                        last = nc.tensor.matmul(last_h(c) if apart else h_ps[:, c, :],
                                                W1_sb[:, k, c * P:(c + 1) * P], uT[:, k, :],
                                                start=(k == 0), stop=(k == C - 1))
                    if c == C - 1:
                        last.then_inc(h_summed, 1)
                    elif apart:
                        last.then_inc(h_part_summed, 1)

            def idle_products(to, times):
                for _ in range(times):
                    nc.tensor.matmul(to, onehot_bf[:, 0, 0:2, :].rearrange("p t n -> p (t n)"),
                                     onehot_bf[:, 1, 0:8, :].rearrange("p t n -> p (t n)"), start=True, stop=True)

            pe.wait_ge(flag_ready, 1)
            slow = pe.value_load(flag[0:1, 0:1], min_val=0, max_val=1)
            with pe.Fori(0, L) as l:
                with pe.If(slow == 0):
                    with pe.Fori(0, BLOCKS - 1) as i:
                        sum_pair(FULL, 0, l, i)
                        sum_pair(FULL, 1, l, i)
                        with pe.If(l == 0):
                            place_w(i + 2, placements[:5])
                        close_block(BLOCKS * l + i)
                        with pe.If(l == 0):
                            place_w(i + 2, placements[5:])
                        product_h(BLOCKS * l + i, l)
                    i = BLOCKS - 1
                    sum_pair(FINAL, 0, l, i)
                    sum_pair(FINAL, 1, l, i)
                    idle_products(y_ps[2][:, :], GAP)
                    close_block(BLOCKS * l + i)
                    idle_products(y_ps[2][:, :], GAP)
                    product_h(BLOCKS * l + i, l, apart=True)
                with pe.Else():
                    with pe.Fori(0, T) as t:
                        for b in range(BLOCKS):
                            pe.wait_ge(slow_onehot, BLOCKS * (T * l + t) + b + 1)
                            nc.tensor.matmul(y_ps[0][:, :], onehot_block[:, :], rows[:, 1, :],
                                             start=True, stop=True).then_inc(slow_summed, 1)
                    with pe.Fori(0, BLOCKS) as i:
                        open_block(BLOCKS * l + i, l, i, False)
                        product_h(BLOCKS * l + i, l)
                idle_products(uT_ps[:, :, :].rearrange("p c n -> p (c n)"), WARM)
                for k, (m, c) in enumerate(HR_ORDER[:-C]):
                    if m < 3 and c == 0:
                        if m + 1 < C - 1:
                            pe.wait_ge(h_part_copied, (C - 1) * l + m + 2)
                        else:
                            pe.wait_ge(h_copied, BLOCKS * (l + 1) + 1)
                    if m < AHEAD:
                        pe.wait_ge(hr_ready, C * BLOCKS * l + k + 1)
                    elif c == 0:
                        pe.wait_ge(hr_ready, C * (BLOCKS * l + m + 1))
                    if m >= 3 and c == 0:
                        pe.wait_ge(y_added, BLOCKS * l + m - 2)
                    at = GUARD - MARGIN + P * ORDER[m]
                    last = nc.tensor.matmul(y_ps[m % 3][:, :], hT[:, c, at:at + P], W2_sb[:, c, :],
                                            start=(c == 0), stop=(c == C - 1))
                    if c == C - 1:
                        last.then_inc(y_summed, 1)
                pe.wait_ge(hr_ready, C * BLOCKS * (l + 1))
                at = GUARD - MARGIN + P * ORDER[-1]
                for h, f in enumerate(HALVES):
                    pe.wait_ge(y_added, BLOCKS * (l + 1) - 3 + h)
                    for c in range(C):
                        last = nc.tensor.matmul(y_half(h), hT[:, c, at:at + P], W2_sb[:, c, f],
                                                start=(c == 0), stop=(c == C - 1))
                    last.then_inc(y_summed if h else half_summed, 1)
                pe.wait_ge(y_summed, BLOCKS * (l + 1))
                pe.sem_inc(params_free, 1)


def kernel(**inputs):
    import concourse.bacc as bacc
    from concourse.bass_utils import run_bass_kernel_spmd

    P, STEP, MARGIN = 128, 32, 16
    x = np.asarray(inputs["x"])
    N, D = x.shape
    src, dst, w = (np.asarray(inputs[k]).reshape(-1) for k in ("src", "dst", "edge_weight1"))
    blocks = -(-(N + MARGIN) // P)
    edges = blocks * STEP * P

    def padded(a, size, fill, before=0):
        out = np.full((size,) + a.shape[1:], fill, a.dtype)
        out[before:before + a.shape[0]] = a
        return out

    def by_tile(a, fill):
        return np.ascontiguousarray(padded(a, edges, fill).reshape(-1, P).T)

    We, be, W1, b1, gamma, beta, W2, b2, eps = (
        np.asarray(inputs["L0_gnn_" + k]) for k in ("We", "be", "W1", "b1", "gamma", "beta", "W2", "b2", "eps"))
    L = W1.shape[0]
    vectors = np.stack([v.reshape(L, D // P, P).transpose(0, 2, 1) for v in (b1, gamma, beta)], axis=2)
    arrays = {
        "x_pad": padded(x, blocks * P, 0, before=MARGIN),
        "src_t": by_tile(src, 0),
        "src_late": np.ascontiguousarray(
            padded(src, edges, 0).reshape(blocks, STEP, P)[:-1, -1].reshape(1, -1)),
        "dst_t": by_tile(dst, N),
        "w_t": by_tile(w, 0),
        "We": padded(We.reshape(L, D), L + 1, 0),
        "be": padded(be, L + 1, 0),
        "W1": W1, "W2": W2, "b2": b2,
        "vectors": np.ascontiguousarray(vectors),
        "eps": eps.reshape(L, 1),
    }
    nc = bacc.Bacc("TRN2", target_bir_lowering=False, num_devices=1)
    args = [nc.dram_tensor(name, a.shape, mybir.dt.from_np(a.dtype), kind="ExternalInput").ap()
            for name, a in arrays.items()]
    out = nc.dram_tensor("out", (N, D), mybir.dt.float32, kind="ExternalOutput").ap()
    gnn_layers(nc, *args, out)
    result = run_bass_kernel_spmd(nc, [arrays], core_ids=[0])
    return result.results[0]["out"]
```
